# Optimizing a Trainium2 kernel written in Bass

```python
import numpy as np
import jax
import jax.numpy as jnp

def _softmax(x, axis=-1):
    return jax.nn.softmax(x, axis=axis)

def _gelu(x):
    return jax.nn.gelu(x, approximate=True)

def _silu(x):
    return jax.nn.silu(x)

def _sigmoid(x):
    return jax.nn.sigmoid(x)

def _layernorm(x, axis=-1, eps=1e-05):
    m = jnp.mean(x, axis=axis, keepdims=True)
    v = jnp.var(x, axis=axis, keepdims=True)
    return (x - m) / jnp.sqrt(v + eps)

def _scatter_add(tgt, idx, src, axis=0):
    return tgt.at[idx].add(src)

def _segment_sum(src, seg, n):
    return jax.ops.segment_sum(src, seg, n)
kernel_name = 'mk_seq_postln_d1_jaxref_r4_b59cee'

def setup_inputs(seed: int=0):
    np.random.seed(seed)
    _w = jnp.asarray

    def _L0_attn_setup():
        import jax, jax.numpy as jnp
        import numpy as np
        IN_FEATURES = 512
        HEAD_NUM = 64
        D = IN_FEATURES // HEAD_NUM
        SCALE = float(np.sqrt(D))
        key = jax.random.key(seed)
        ks = jax.random.split(key, 9)
        F = IN_FEATURES
        x = jax.random.normal(ks[0], (4, 256, F), dtype=jnp.float32)
        w = lambda k: jax.random.normal(k, (F, F), dtype=jnp.float32) * 0.02
        b = lambda k: jax.random.normal(k, (F,), dtype=jnp.float32) * 0.01
        return {'x': x, 'Wq': w(ks[1]), 'bq': b(ks[2]), 'Wk': w(ks[3]), 'bk': b(ks[4]), 'Wv': w(ks[5]), 'bv': b(ks[6]), 'Wo': w(ks[7]), 'bo': b(ks[8])}
    _L0_attn_in = _L0_attn_setup()

    def _L0_ffn_setup():
        import jax, jax.numpy as jnp
        import numpy as np
        TOPK = 6
        CAP = 256
        ROUTE_SCALE = 1.0
        key = jax.random.key(seed)
        k = jax.random.split(key, 6)
        B, T, C = (2, 512, 512)
        E, H, HS = (64, 64, 128)
        std = 0.01
        return {'x': jax.random.normal(k[0], (B, T, C), jnp.float32), 'w_gate': jax.random.normal(k[1], (C, E), jnp.float32) * std, 'w_shared_up': jax.random.normal(k[2], (C, 2 * HS), jnp.float32) * std, 'w_shared_down': jax.random.normal(k[3], (HS, C), jnp.float32) * std, 'w_up': jax.random.normal(k[4], (E, C, 2 * H), jnp.float32) * std, 'w_down': jax.random.normal(k[5], (E, H, C), jnp.float32) * std}
    _L0_ffn_in = _L0_ffn_setup()
    _d = {'L0_attn_x': _L0_attn_in['x'], 'L0_attn_Wq': _L0_attn_in['Wq'], 'L0_attn_bq': _L0_attn_in['bq'], 'L0_attn_Wk': _L0_attn_in['Wk'], 'L0_attn_bk': _L0_attn_in['bk'], 'L0_attn_Wv': _L0_attn_in['Wv'], 'L0_attn_bv': _L0_attn_in['bv'], 'L0_attn_Wo': _L0_attn_in['Wo'], 'L0_attn_bo': _L0_attn_in['bo'], 'L0_ffn_w_gate': _L0_ffn_in['w_gate'], 'L0_ffn_w_shared_up': _L0_ffn_in['w_shared_up'], 'L0_ffn_w_shared_down': _L0_ffn_in['w_shared_down'], 'L0_ffn_w_up': _L0_ffn_in['w_up'], 'L0_ffn_w_down': _L0_ffn_in['w_down']}
    _x0 = _d['L0_attn_x']
    _d['L0_attn_x'] = jax.random.normal(jax.random.fold_in(jax.random.key(seed), 1), (1, 2048, 512), dtype=_x0.dtype)
    del _x0
    return _d

def reference(L0_attn_x, L0_attn_Wq, L0_attn_bq, L0_attn_Wk, L0_attn_bk, L0_attn_Wv, L0_attn_bv, L0_attn_Wo, L0_attn_bo, L0_ffn_w_gate, L0_ffn_w_shared_up, L0_ffn_w_shared_down, L0_ffn_w_up, L0_ffn_w_down):

    def _L0_attn_ref(x, Wq, bq, Wk, bk, Wv, bv, Wo, bo):
        import jax, jax.numpy as jnp
        import numpy as np
        IN_FEATURES = 512
        HEAD_NUM = 64
        D = IN_FEATURES // HEAD_NUM
        SCALE = float(np.sqrt(D))
        B, S, F = x.shape
        d = D
        h = F // d
        q = x @ Wq + bq
        k = x @ Wk + bk
        v = x @ Wv + bv

        def to_heads(t):
            return t.reshape(B, S, d, h).transpose(0, 2, 1, 3)
        q, k, v = (to_heads(q), to_heads(k), to_heads(v))
        scores = jnp.einsum('bdsh,bdth->bdst', q, k) / SCALE
        weights = jax.nn.softmax(scores, axis=-1)
        feats = jnp.einsum('bdst,bdth->bdsh', weights, v)
        feats = feats.transpose(0, 2, 1, 3).reshape(B, S, F)
        return feats @ Wo + bo

    def _L0_ffn_ref(x, w_gate, w_shared_up, w_shared_down, w_up, w_down):
        import jax, jax.numpy as jnp
        import numpy as np
        TOPK = 6
        CAP = 256
        ROUTE_SCALE = 1.0
        B, T, C = x.shape
        E = w_gate.shape[1]
        x_flat = x.reshape(-1, C)
        N = x_flat.shape[0]
        su = x_flat @ w_shared_up
        y_s, g_s = jnp.split(su, 2, axis=-1)
        shared = jax.nn.silu(g_s) * y_s @ w_shared_down
        scores = jax.nn.sigmoid(x_flat @ w_gate)
        _, topk_idx = jax.lax.top_k(scores, TOPK)
        w = jnp.take_along_axis(scores, topk_idx, axis=-1)
        w = w / w.sum(-1, keepdims=True) * ROUTE_SCALE
        flat_e = topk_idx.reshape(-1)
        oh = jax.nn.one_hot(flat_e, E, dtype=jnp.int32)
        pos = jnp.take_along_axis(jnp.cumsum(oh, axis=0), flat_e[:, None], axis=1)[:, 0] - 1
        valid = pos < CAP
        pos_c = jnp.where(valid, pos, CAP - 1)
        token_ids = jnp.repeat(jnp.arange(N), TOPK)
        x_disp = jnp.zeros((E, CAP, C), x.dtype).at[flat_e, pos].set(x_flat[token_ids], mode='drop')
        up = jnp.einsum('ecd,edh->ech', x_disp, w_up)
        g_r, v_r = jnp.split(up, 2, axis=-1)
        h_r = jax.nn.silu(g_r) * v_r
        out_r = jnp.einsum('ech,ehd->ecd', h_r, w_down)
        y_ts = out_r[flat_e, pos_c]
        y_ts = jnp.where(valid[:, None], y_ts, 0.0)
        routed = (y_ts.reshape(N, TOPK, C) * w[:, :, None]).sum(axis=1)
        return (shared + routed).reshape(B, T, C)
    x = L0_attn_x
    x = _layernorm(x + _L0_attn_ref(x, L0_attn_Wq, L0_attn_bq, L0_attn_Wk, L0_attn_bk, L0_attn_Wv, L0_attn_bv, L0_attn_Wo, L0_attn_bo), axis=-1)
    x = _layernorm(x + _L0_ffn_ref(x, L0_ffn_w_gate, L0_ffn_w_shared_up, L0_ffn_w_shared_down, L0_ffn_w_up, L0_ffn_w_down), axis=-1)
    return x

_drawn_inputs = setup_inputs


def setup_inputs(seed=0):
    import zlib

    import numpy as np

    out = dict(_drawn_inputs(seed))
    spreads = {}
    factors = {'L0_attn_Wq': 8.0,
     'L0_attn_bq': 8.0,
     'L0_attn_Wk': 8.0,
     'L0_attn_bk': 8.0,
     'L0_attn_Wv': 7.693,
     'L0_attn_bv': 8.0,
     'L0_attn_Wo': 6.288,
     'L0_attn_bo': 5.907,
     'L0_ffn_w_gate': 8.0,
     'L0_ffn_w_shared_up': 8.0,
     'L0_ffn_w_shared_down': 8.0,
     'L0_ffn_w_up': 8.0,
     'L0_ffn_w_down': 8.0}
    for name, (base, spread) in spreads.items():
        noise = np.random.default_rng([zlib.crc32(name.encode()), seed]).standard_normal(out[name].shape)
        drawn = base * np.exp(spread * noise) if base else spread * noise
        out[name] = jnp.asarray(drawn.astype(out[name].dtype))
    for name, factor in factors.items():
        out[name] = (out[name] * factor).astype(out[name].dtype)
    return out
```

```python
from contextlib import ExitStack

import numpy as np

import concourse.bass as bass
from concourse import mybir

F32 = mybir.dt.float32
F32R = mybir.dt.float32r
BF16 = mybir.dt.bfloat16
U32 = mybir.dt.uint32
ALU = mybir.AluOpType
ACT = mybir.ActivationFunctionType
AX = mybir.AxisListType

P = 128
BANK = 512


class Counter:

    def __init__(self, handle):
        self.handle, self.count = handle, 0

    def add(self, n):
        self.count += n
        return (self, self.count)


class Queue:

    def __init__(self):
        self.ops, self.seen = [], {}

    def wait(self, *marks):
        for mark in marks:
            if mark is None:
                continue
            counter, value = mark
            if self.seen.get(id(counter), 0) < value:
                self.seen[id(counter)] = value
                self.ops.append(lambda e, h=counter.handle, v=value: e.wait_ge(h, v))

    def do(self, op, counter=None, by=1):
        if counter is None:
            self.ops.append(op)
            return None
        self.ops.append(lambda e, h=counter.handle: op(e).then_inc(h, by))
        return counter.add(by)

    def run(self, e):
        for op in self.ops:
            op(e)


def build(nc, x, Wq, bq, Wk, bk, Wv, bv, Wo, bo, w_gate, w_sup, w_sdown, w_up, w_down, out):
    _, T, C = x.shape
    D = 64
    H = C // D
    SCALE = float(np.sqrt(8.0))
    E = w_gate.shape[1]
    HE = w_down.shape[1]
    HS = w_sdown.shape[0]
    TOPK, CAP, EPS = 6, 256, 1e-5
    KC = C // P
    NT = T // P
    QC = 256
    QT = QC // P
    NCH = T // QC
    HALF = T // 2
    KT4 = T // P // 4
    SKIP = 1 << 17

    ctx = ExitStack()
    with ctx:
        def sb(name, shape, dt=F32, stack=ctx):
            return stack.enter_context(nc.sbuf_tensor(name, shape, dt))

        def counter(name):
            return Counter(ctx.enter_context(nc.semaphore(name)))

        def hbm(name, shape, dt=F32):
            return nc.dram_tensor(name, shape, dt).ap()

        q_hbm = hbm("q_hbm", (H // 2, 2, P, T))
        x1_hbm = hbm("x1_hbm", (T, C))
        disp_hbm = hbm("disp_hbm", (E * CAP, C))
        y_hbm = hbm("y_hbm", (E * CAP, C))

        slots = [ctx.enter_context(nc.psum_tensor(f"slot{i}", [P, 2 * BANK], F32)) for i in range(3)]
        pv_acc = ctx.enter_context(nc.psum_tensor("pv_acc", [P, BANK], F32))
        misc = ctx.enter_context(nc.psum_tensor("misc", [P, BANK], F32))
        slot_free = [[], [], []]
        slot_turn = [0]

        def take_slot():
            i = slot_turn[0] % 3
            slot_turn[0] += 1
            return i, slots[i]

        ident = sb("ident", [P, P])
        slot_of = sb("slot_of", [P, NT, TOPK], U32)
        weight_of = sb("weight_of", [P, NT, TOPK])
        half_neg = sb("half_neg", [P, 1])
        att = ExitStack()
        k_stack = sb("k_stack", [P, H, T], F32R, att)
        v_pair = sb("v_pair", [P, NT, H, P], F32R, att)
        wo_sb = sb("wo_sb", [P, KC, C], F32, att)
        wg_sb = sb("wg_sb", [P, KC, E], F32, att)
        bo_all = sb("bo_all", [P, C], F32, att)
        before = sb("before", [P, P], BF16, att)
        ones_bf = sb("ones_bf", [P, P], BF16, att)
        iota_e = sb("iota_e", [P, E], F32, att)
        count_so_far = sb("count_so_far", [P, E], BF16, att)
        pro = ExitStack()
        x_t = sb("x_t", [P, KC, T], F32, pro)
        w_in = [sb(f"w_in{i}", [P, KC, C], F32, pro) for i in range(2)]
        stage = [sb(f"stage{i}", [P, 2, C], F32, pro) for i in range(2)]
        q_hi = sb("q_hi", [P, 2 * BANK], F32R, pro)
        q_lo = sb("q_lo", [P, 2 * BANK], F32R, pro)
        zeros = sb("zeros", [P, C // 2], F32, pro)
        bias_k = sb("bias_k", [P, KC], F32, pro)
        bias_q = sb("bias_q", [P, KC], F32, pro)
        pro.close()
        prob = sb("prob", [P, 2, QT, T], F32, att)
        p_hi = [sb(f"p_hi{i}", [P, 4, QC], F32R, att) for i in range(2)]
        p_lo = [sb(f"p_lo{i}", [P, 4, QC], F32R, att) for i in range(2)]
        q_stack = [sb(f"q_stack{i}", [P, 2, QC], F32R, att) for i in range(2)]
        row_min = sb("row_min", [P, 2, QT, 2], F32, att)
        row_sum = sb("row_sum", [P, 2, QT, 2], F32, att)
        row_inv = sb("row_inv", [P, QT], F32, att)
        scaled = sb("scaled", [P, QC], F32, att)
        moved = sb("moved", [P, QC], F32, att)
        feats = sb("feats", [P, H // 2, QC], F32, att)
        resid = [sb(f"resid{i}", [P, C], F32, att) for i in range(QT)]
        x1 = sb("x1", [P, C], F32, att)
        x1_t = sb("x1_t", [P, KC, P], F32, att)
        small = sb("small", [P, 16], F32, att)
        stats, mean_var, rstd, top_sum, top_f = (small[:, a:b] for a, b in ((0, 6), (6, 8), (8, 9), (9, 10), (10, 16)))
        score = sb("score", [P, E], F32, att)
        top = sb("top", [P, 8], F32, att)
        top_i = sb("top_i", [P, 8], U32, att)
        onehot = x1_t[:, 0:TOPK * E // P, :].rearrange("p a b -> p (a b)").rearrange("p (k e) -> p k e", e=E)
        picked = sb("picked", [P, E], BF16, att)
        place, over, slot_f = (x1_t[:, KC - 1, 8 * i:8 * i + TOPK] for i in range(3))
        scat = sb("scat", [P, TOPK], U32, att)
        att.close()
        NB, NY = 5, 3
        rows = [sb(f"rows{i}", [P, 2, C]) for i in range(NB)]
        up_w = [sb(f"up_w{i}", [P, KC, 2 * HE]) for i in range(NB)]
        down_w = [sb(f"down_w{i}", [HE, C]) for i in range(NB)]
        sup_w = sb("sup_w", [P, KC, 2 * HS])
        sdown_w = sb("sdown_w", [HS, C])
        rows_t = [sb(f"rows_t{i}", [P, KC, CAP]) for i in range(2)]
        gate_e = [sb(f"gate_e{i}", [P, CAP]) for i in range(2)]
        gate_g = [sb(f"gate_g{i}", [P, CAP]) for i in range(2)]
        hid = [sb(f"hid{i}", [P, CAP]) for i in range(2)]
        y_out = [sb(f"y_out{i}", [P, 2, C]) for i in range(NY)]
        base = sb("base", [P, NT, C])
        NG = 18
        got = [sb(f"got{i}", [P, C]) for i in range(NG)]
        f_stats = sb("f_stats", [P, 2, 6])
        f_mv = sb("f_mv", [P, 2, 2])
        f_rstd = sb("f_rstd", [P, 2])
        final = [sb(f"final{i}", [P, C]) for i in range(2)]

        pe, act, dve, pool, sp = Queue(), Queue(), Queue(), Queue(), Queue()

        c_pe = {n: counter(f"pe_{n}") for n in ("fill", "scores", "turned", "pv", "misc")}
        c_act = {n: counter(f"act_{n}") for n in ("hi", "exp", "misc")}
        c_dve = {n: counter(f"dve_{n}") for n in ("min", "lo", "chain")}
        c_pool = {n: counter(f"pool_{n}") for n in ("const", "chain")}
        d = {n: counter(f"dma_{n}") for n in (
            "wk", "wq", "wv", "bias", "bv", "once", "zero", "qst", "moved", "feats", "resid0", "resid1", "sup", "x0", "x1_",
            "q0", "q1", "st", "r0", "r1", "r2", "r3", "r4", "y0", "y1", "y2", "o0", "o1")}
        d_got = [counter(f"dma_got{i}") for i in range(NG)]

        def chain(op):
            dve.wait((c_dve["chain"], c_dve["chain"].count))
            return dve.do(op, c_dve["chain"])

        def pool_chain(op):
            pool.wait((c_pool["chain"], c_pool["chain"].count))
            return pool.do(op, c_pool["chain"])

        def bank_product(dst, pairs, start=True, stop=True):
            for n, (a, b) in enumerate(pairs[:-1]):
                pe.do(lambda e, a=a, b=b, n=n: e.matmul(dst, a, b, start=start and n == 0, stop=False))
            a, b = pairs[-1]
            return lambda e: e.matmul(dst, a, b, start=start and len(pairs) == 1, stop=stop)

        pool.do(lambda e: e.memset(ident[:, :], 0.0), c_pool["const"])
        pool.wait((c_pool["const"], 1))
        ident_ready = pool.do(lambda e: e.affine_select(
            out=ident[:, :], in_=ident[:, :], compare_op=ALU.not_equal, fill=1.0, base=0,
            pattern=[[-1, P]], channel_multiplier=1), c_pool["const"])
        zeros_ready = pool.do(lambda e: e.memset(zeros[:, :], 0.0), c_pool["const"])
        pool.do(lambda e: e.memset(half_neg[:, :], -0.5))
        pool.do(lambda e: e.memset(count_so_far[:, :], 0.0))
        pool.do(lambda e: e.iota(iota_e[:, :], [[1, E]], base=0, channel_multiplier=0,
                                 allow_small_or_imprecise_dtypes=True))
        ones_ready = pool.do(lambda e: e.memset(ones_bf[:, :], 1.0), c_pool["const"])
        pool.wait(ones_ready)
        consts = pool.do(lambda e: e.affine_select(
            out=before[:, :], in_=ones_bf[:, :], compare_op=ALU.is_gt, fill=0.0, base=0,
            pattern=[[1, P]], channel_multiplier=-1), c_pool["const"])

        def w_view(w):
            return w.rearrange("(k p) n -> p k n", p=P)

        x_rows = x.rearrange("b (g t p) n -> (b g) p t n", t=2, p=P)
        x_landed, x_read = [None] * (NT // 2), [None] * 2
        for g in range(2):
            x_landed[g] = sp.do(lambda e, g=g: e.dma_start(stage[g][:, :, :], x_rows[g]), d[("x0", "x1_")[g]], 16)
        wk_in = sp.do(lambda e: e.dma_start(w_in[0][:, :, :], w_view(Wk)), d["wk"], 16)
        for b, t in ((bk, bias_k), (bq, bias_q)):
            bias_in = sp.do(lambda e, b=b, t=t: e.dma_start(t[:, :], b), d["bias"], 16)
        wq_in = sp.do(lambda e: e.dma_start(w_in[1][:, :, :], w_view(Wq)), d["wq"], 16)

        turned = None
        for g in range(NT // 2):
            if g >= 2:
                sp.wait(x_read[g % 2])
                x_landed[g] = sp.do(lambda e, g=g: e.dma_start(stage[g % 2][:, :, :], x_rows[g]),
                                    d[("x0", "x1_")[g % 2]], 16)
            i, slot = take_slot()
            view = slot[:, :].rearrange("p (t k q) -> p t k q", t=2, k=KC)
            pe.wait(ident_ready, x_landed[g], *slot_free[i])
            for t in range(2):
                for k in range(KC):
                    last = (lambda e, g=g, t=t, k=k, view=view: e.transpose(
                        view[:, t, k, :], stage[g % 2][:, t, k * P:(k + 1) * P], ident[:, :]))
                    if (t, k) == (1, KC - 1):
                        x_read[g % 2] = pe.do(last, c_pe["fill"])
                    else:
                        pe.do(last)
            dst = x_t[:, :, g * 2 * P:(g + 1) * 2 * P].rearrange("p k (t q) -> p k t q", t=2)
            src = slot[:, :].rearrange("p (t k q) -> p k t q", t=2, k=KC)
            if g % 2:
                act.wait(x_read[g % 2])
                for k in range(KC):
                    turned_a = act.do(lambda e, dst=dst, src=src, k=k: e.activation(dst[:, k], src[:, k], ACT.Copy),
                                      c_act["misc"])
                slot_free[i] = [turned_a]
            else:
                dve.wait(x_read[g % 2])
                turned_d = dve.do(lambda e, dst=dst, src=src: e.tensor_copy(dst, src), c_dve["chain"])
                slot_free[i] = [turned_d]

        sp.wait(zeros_ready)
        zero_row = zeros[:, :].unsqueeze(1).to_broadcast([P, 4, C // 2])
        disp_pieces = disp_hbm.rearrange("(g p t) (u n) -> g p (t u) n", p=P, t=2, u=2)
        zero_pieces = [lambda e, g=g: e.dma_start(disp_pieces[g], zero_row) for g in range(E * CAP // (P * 2))]

        def zero_some(count):
            for _ in range(count):
                if zero_pieces:
                    sp.do(zero_pieces.pop(0), d["zero"], 16)

        q_stored = None
        for name, w, w_landed, bias in (("k", w_in[0], wk_in, bias_k), ("q", w_in[1], wq_in, bias_q)):
            for pair in range(H // 2):
                for g in range(T // (2 * BANK)):
                    tok = slice(g * 2 * BANK, (g + 1) * 2 * BANK)
                    i, slot = take_slot()
                    pe.wait(w_landed, turned_a, turned_d, *slot_free[i])
                    for n in range(2):
                        cols = slice(g * 2 * BANK + n * BANK, g * 2 * BANK + (n + 1) * BANK)
                        last = bank_product(slot[:, n * BANK:(n + 1) * BANK], [
                            (w[:, k, pair * P:(pair + 1) * P], x_t[:, k, cols]) for k in range(KC)])
                        made = pe.do(last, c_pe["fill"])
                    if name == "k":
                        zero_some(4)
                        for odd in range(2):
                            h, hi, lo = 2 * pair + odd, slice(odd * D, (odd + 1) * D), slice((1 - odd) * D, (2 - odd) * D)
                            act.wait(made, bias_in)
                            rounded = act.do(lambda e, h=h, hi=hi, slot=slot, tok=tok, bias=bias, pair=pair: e.activation(
                                k_stack[hi, h, tok], slot[hi, :], ACT.Identity, bias=bias[hi, pair:pair + 1]), c_act["hi"])
                            dve.wait(rounded)
                            slot_free[i] = [dve.do(lambda e, h=h, hi=hi, lo=lo, slot=slot, tok=tok, bias=bias, pair=pair:
                                                  e.scalar_tensor_tensor(
                                out=k_stack[lo, h, tok], in0=slot[hi, :], scalar=bias[hi, pair:pair + 1],
                                in1=k_stack[hi, h, tok].bitcast(F32), op0=ALU.add, op1=ALU.subtract), c_dve["lo"])]
                    else:
                        act.wait(made, bias_in, q_stored)
                        rounded = act.do(lambda e, slot=slot, bias=bias, pair=pair: e.activation(
                            q_hi[:, :], slot[:, :], ACT.Identity, bias=bias[:, pair:pair + 1]), c_act["hi"])
                        dve.wait(rounded)
                        slot_free[i] = [dve.do(lambda e, slot=slot, bias=bias, pair=pair: e.scalar_tensor_tensor(
                            out=q_lo[:, :], in0=slot[:, :], scalar=bias[:, pair:pair + 1],
                            in1=q_hi[:, :].bitcast(F32), op0=ALU.add, op1=ALU.subtract), c_dve["lo"])]
                        sp.wait(*slot_free[i])
                        for part, src in ((0, q_hi), (1, q_lo)):
                            q_stored = sp.do(lambda e, src=src, part=part, pair=pair, tok=tok: e.dma_start(
                                q_hbm[pair, part, :, tok], src[:, :].bitcast(F32)), d["qst"], 16)
            if name == "k":
                sp.wait(made)
                wv_in = sp.do(lambda e: e.dma_start(w_in[0][:, :, :], w_view(Wv)), d["wv"], 16)
                bv_all = stage[0][:, 0, :]
                bv_in = sp.do(lambda e: e.dma_start(bv_all, bv.partition_broadcast(P)), d["bv"], 16)
                for a, b in ((wo_sb[:, :, :], w_view(Wo)), (wg_sb[:, :, :], w_view(w_gate)),
                             (bo_all[:, :], bo.partition_broadcast(P))):
                    once_in = sp.do(lambda e, a=a, b=b: e.dma_start(a, b), d["once"], 16)

        v_plain = stage[1]
        for g in range(NT // 2):
            zero_some(4)
            i, slot = take_slot()
            pe.wait(wv_in, *slot_free[i])
            for t in range(2):
                last = bank_product(slot[:, t * BANK:(t + 1) * BANK], [
                    (x_t[:, k, (2 * g + t) * P:(2 * g + t + 1) * P], w_in[0][:, k, :]) for k in range(KC)])
                made = pe.do(last, c_pe["fill"])
            dve.wait(made, bv_in, (c_pool["chain"], c_pool["chain"].count), (c_act["hi"], c_act["hi"].count))
            added = dve.do(lambda e, slot=slot: e.tensor_tensor(
                v_plain[:, :, :], slot[:, :].rearrange("p (t n) -> p t n", t=2),
                bv_all.unsqueeze(1).to_broadcast([P, 2, C]), ALU.add), c_dve["chain"])
            slot_free[i] = [added]
            act.wait(added)
            for t in range(2):
                src = v_plain[:, t, :].rearrange("p (h c) -> p h c", h=H)
                rounded = act.do(lambda e, g=g, t=t, src=src: e.activation(
                    v_pair[:, 2 * g + t, :, 0:D], src, ACT.Copy), c_act["hi"])
            pool.wait(rounded)
            for t in range(2):
                src = v_plain[:, t, :].rearrange("p (h c) -> p h c", h=H)
                v_made = pool_chain(lambda e, g=g, t=t, src=src: e.tensor_tensor(
                    v_pair[:, 2 * g + t, :, D:P], src, v_pair[:, 2 * g + t, :, 0:D].bitcast(F32), ALU.subtract))

        def phase_end():
            marks = [(c, c.count) for c in (*c_pe.values(), *c_act.values(), *c_dve.values(), *c_pool.values(),
                                            *d.values()) if c.count]
            for q in (pe, act, dve, pool, sp):
                q.wait(*marks)

        phase_end()

        groups = [(c, h) for c in range(NCH) for h in range(H)]
        q_in, q_read = {}, [None] * 2
        lowest, exp_done, t_read, hi_done, lo_done, pv_read = {}, {}, {}, [None] * 2, [None] * 2, [None] * 2
        misc_free = [None]
        pv_free = [None]

        def load_q(m):
            c, h = groups[m]
            sp.wait(q_read[m % 2])
            src = q_hbm[h // 2, :, (h % 2) * D:(h % 2 + 1) * D, c * QC:(c + 1) * QC].rearrange("s c q -> c s q")
            for half in (slice(0, D), slice(D, P)):
                q_in[m] = sp.do(lambda e, half=half: e.dma_start(q_stack[m % 2][half, :, :].bitcast(F32), src),
                                d[f"q{m % 2}"], 16)

        def scores(m, u):
            c, h = groups[m]
            half, j = divmod(u, QT)
            i, slot = take_slot()
            pe.wait(q_in[m], *slot_free[i])
            qs = q_stack[m % 2]
            for part in range(2):
                for n in range(2):
                    keys = slice(half * HALF + n * BANK, half * HALF + (n + 1) * BANK)
                    op = (lambda e, part=part, n=n, keys=keys: e.matmul(
                        slot[:, n * BANK:(n + 1) * BANK], qs[:, part, j * P:(j + 1) * P], k_stack[:, h, keys],
                        start=part == 0, stop=part == 1))
                    if (part, n) == (1, 1):
                        made = pe.do(op, c_pe["scores"])
                    else:
                        pe.do(op)
            q_read[m % 2] = made
            dve.wait(made, t_read.get((m - 2, half)))
            first = 3.0e38 if half == 0 else row_min[:, m % 2, j, 0:1]
            if half:
                dve.wait((c_dve["min"], c_dve["min"].count))
            low = dve.do(lambda e: e.tensor_scalar(
                prob[:, m % 2, j, half * HALF:(half + 1) * HALF], slot[:, :], -1.0 / SCALE, first, ALU.mult, ALU.min,
                accum_out=row_min[:, m % 2, j, half:half + 1]), c_dve["min"])
            slot_free[i] = [low]
            lowest[m, j] = low

        def raise_exp(m, u):
            half, j = divmod(u, QT)
            act.wait(lowest[m, j])
            exp_done[m, j, half] = act.do(lambda e: e.activation(
                prob[:, m % 2, j, half * HALF:(half + 1) * HALF], prob[:, m % 2, j, half * HALF:(half + 1) * HALF],
                ACT.Exp, bias=row_min[:, m % 2, j, 1:2], scale=-1.0,
                accum_out=row_sum[:, m % 2, j, half:half + 1]), c_act["exp"])

        def turn(m, u):
            i, slot = take_slot()
            view = slot[:, :].rearrange("p (t q) -> p t q", t=4)
            pe.wait(*slot_free[i], *(exp_done[m, j, u // 2] for j in range(QT)))
            for t in range(4):
                for j in range(QT):
                    op = (lambda e, t=t, j=j: e.transpose(
                        view[:, t, j * P:(j + 1) * P], prob[:, m % 2, j, (4 * u + t) * P:(4 * u + t + 1) * P],
                        ident[:, :]))
                    if (t, j) == (3, QT - 1):
                        made = pe.do(op, c_pe["turned"])
                    else:
                        pe.do(op)
            t_read[m, u // 2] = made
            b = u % 2
            act.wait(made, pv_read[b])
            hi_done[b] = act.do(lambda e: e.activation(p_hi[b][:, :, :], view, ACT.Copy), c_act["hi"])
            return i, view

        def split_lo(u, i, view):
            b = u % 2
            dve.wait(hi_done[b])
            lo_done[b] = dve.do(lambda e: e.tensor_tensor(
                p_lo[b][:, :, :], view, p_hi[b][:, :, :].bitcast(F32), ALU.subtract), c_dve["lo"])
            slot_free[i] = [lo_done[b]]

        def times_v(m, u):
            c, h = groups[m]
            b = u % 2
            pe.wait(hi_done[b], lo_done[b])
            if u == 0:
                pe.wait(pv_free[0])
            for t in range(4):
                for part, src in enumerate((p_hi[b], p_lo[b])):
                    kt = 4 * u + t
                    op = (lambda e, kt=kt, t=t, part=part, src=src: e.matmul(
                        pv_acc[:, 0:QC], v_pair[:, kt, h, :], src[:, t, :], start=kt == 0 and part == 0,
                        stop=kt == NT - 1 and part == 1))
                    if (t, part) == (3, 1):
                        pv_read[b] = pe.do(op, c_pe["pv"])
                    else:
                        pe.do(op)

        inv_done = {}

        inverted = {}

        def invert_sums(m):
            dve.wait(*(exp_done[m, j, 1] for j in range(QT)))
            chain(lambda e: e.tensor_tensor(row_inv[:, :], row_sum[:, m % 2, :, 0], row_sum[:, m % 2, :, 1], ALU.add))
            inverted[m] = chain(lambda e: e.reciprocal(row_inv[:, :], row_inv[:, :]))

        def spread_inverse(m):
            pe.wait(inverted[m], misc_free[0])
            for j in range(QT):
                made = pe.do(lambda e, j=j: e.matmul(
                    misc[:, j * P:(j + 1) * P], row_inv[:, j:j + 1].to_broadcast([P, P]), ident[:, :],
                    start=True, stop=True), c_pe["misc"])
            act.wait(made, feats_done.get(m - 1))
            inv_done[m] = act.do(lambda e: e.activation(scaled[:, :], misc[:, 0:QC], ACT.Copy), c_act["misc"])
            misc_free[0] = inv_done[m]

        feats_read, feats_done, moved_done = [None], {}, [None]

        def finish_group(m):
            c, h = groups[m]
            pair, odd = divmod(h, 2)
            dve.wait(inv_done[m], pv_read[1], moved_done[0])
            pv_free[0] = done = dve.do(lambda e: e.tensor_tensor(
                scaled[:, :], pv_acc[:, 0:QC], scaled[:, :], ALU.mult), c_dve["chain"])
            sp.wait(done)
            lo_in = sp.do(lambda e: e.dma_start(moved[0:D, :], scaled[D:P, :]), d["moved"], 16)
            target = moved[0:D, :] if odd else feats[0:D, pair, :]
            pool.wait(done, lo_in, feats_read[0])
            moved_done[0] = feats_done[m] = pool_chain(lambda e: e.tensor_tensor(
                target, scaled[0:D, :], moved[0:D, :], ALU.add))
            if odd:
                sp.wait(feats_done[m])
                moved_done[0] = feats_done[m] = sp.do(lambda e: e.dma_start(
                    feats[D:P, pair, :], target), d["feats"], 16)

        x_tiles = x.rearrange("b (t p) n -> (b t) p n", p=P)
        x1_stored, scattered = [None], [None]
        scat_counters = [counter("dma_scat")]
        resid_free = [None] * QT

        def chunk_end(c):
            biased, resid_done = {}, {}
            for j in range(QT):
                sp.wait(resid_free[j])
                x_in = sp.do(lambda e, j=j: e.dma_start(resid[j][:, :], x_tiles[c * QT + j]), d[f"resid{j}"], 16)
                pool.wait(x_in)
                biased[j] = pool_chain(lambda e, j=j: e.tensor_tensor(resid[j][:, :], resid[j][:, :], bo_all[:, :], ALU.add))
            yield
            for j in range(QT):
                pe.wait(feats_done[c * H + H - 1], feats_done[c * H + H - 2], misc_free[0])
                made = pe.do(bank_product(misc[:, :], [
                    (feats[:, k, j * P:(j + 1) * P], wo_sb[:, k, :]) for k in range(KC)]), c_pe["misc"])
                feats_read[0] = made
                dve.wait(made, biased[j])
                misc_free[0] = chain(lambda e, j=j: e.tensor_tensor(resid[j][:, :], misc[:, :], resid[j][:, :], ALU.add))
                yield
            for j in range(QT):
                t, res = c * QT + j, resid[j]
                yield
                chain(lambda e, res=res: e.bn_stats(stats[:, :], res[:, :]))
                chain(lambda e: e.bn_aggr(mean_var[:, :], stats[:, :]))
                var = chain(lambda e: e.tensor_scalar(mean_var[:, 1:2], mean_var[:, 1:2], EPS, None, ALU.add))
                pool.wait(var)
                root = pool_chain(lambda e: e.tensor_tensor(rstd[:, :], mean_var[:, 1:2], half_neg[:, :], ALU.pow))
                yield
                dve.wait(root, scattered[0], x1_stored[0])
                normed = resid_free[j] = chain(lambda e, res=res: e.tensor_scalar(
                    x1[:, :], res[:, :], mean_var[:, 0:1], rstd[:, 0:1], ALU.subtract, ALU.mult))
                sp.wait(normed)
                x1_stored[0] = sp.do(lambda e, t=t: e.dma_start(x1_hbm[t * P:(t + 1) * P, :], x1[:, :]),
                                     d["st"], 16)
                pe.wait(normed, misc_free[0])
                for k in range(KC):
                    made = pe.do(lambda e, k=k: e.transpose(
                        misc[:, k * P:(k + 1) * P], x1[:, k * P:(k + 1) * P], ident[:, :]), c_pe["misc"])
                act.wait(made, (c_dve["chain"], c_dve["chain"].count))
                misc_free[0] = flipped = act.do(lambda e: e.activation(
                    x1_t[:, :, :], misc[:, :].rearrange("p (k q) -> p k q", k=KC), ACT.Copy), c_act["misc"])
                yield
                pe.wait(flipped, misc_free[0])
                made = pe.do(bank_product(misc[:, 0:E], [(x1_t[:, k, :], wg_sb[:, k, :]) for k in range(KC)]),
                             c_pe["misc"])
                act.wait(made, (c_dve["chain"], c_dve["chain"].count))
                misc_free[0] = raised = act.do(lambda e: e.activation(score[:, :], misc[:, 0:E], ACT.Exp, scale=-1.0),
                                               c_act["misc"])
                yield
                dve.wait(raised)
                chain(lambda e: e.tensor_scalar(score[:, :], score[:, :], 1.0, None, ALU.add))
                chain(lambda e: e.reciprocal(score[:, :], score[:, :]))
                yield
                chain(lambda e: e.max(top[:, :], score[:, :]))
                chain(lambda e: e.max_index(top_i[:, :], top[:, :], score[:, :]))
                chain(lambda e: e.tensor_copy(top_f[:, :], top_i[:, 0:TOPK]))
                chain(lambda e: e.tensor_reduce(top_sum[:, :], top[:, 0:TOPK], AX.X, ALU.add))
                chain(lambda e: e.reciprocal(top_sum[:, :], top_sum[:, :]))
                yield
                chain(lambda e: e.tensor_tensor(
                    onehot[:, :, :], iota_e[:, :].unsqueeze(1).to_broadcast([P, TOPK, E]),
                    top_f[:, :].unsqueeze(2).to_broadcast([P, TOPK, E]), ALU.is_equal))
                yield
                mask = chain(lambda e: e.tensor_reduce(
                    picked[:, :], onehot[:, :, :].rearrange("p k e -> p e k"), AX.X, ALU.max))
                yield
                pe.wait(mask, misc_free[0], (c_pool["chain"], c_pool["chain"].count))
                made = pe.do(bank_product(misc[:, 0:E], [
                    (before[:, :], picked[:, :]), (ones_bf[:, :], count_so_far[:, :])]), c_pe["misc"])
                pool.wait(made, mask)
                pool_chain(lambda e: e.tensor_tensor(count_so_far[:, :], count_so_far[:, :], picked[:, :], ALU.add))
                dve.wait(made)
                misc_free[0] = chain(lambda e: e.tensor_tensor(
                    onehot[:, :, :], onehot[:, :, :], misc[:, 0:E].unsqueeze(1).to_broadcast([P, TOPK, E]), ALU.mult))
                chain(lambda e: e.tensor_reduce(place[:, :], onehot[:, :, :], AX.X, ALU.add))
                yield
                chain(lambda e: e.tensor_scalar(over[:, :], place[:, :], float(CAP), float(SKIP), ALU.is_ge, ALU.mult))
                chain(lambda e: e.scalar_tensor_tensor(out=slot_f[:, :], in0=top_f[:, :], scalar=float(CAP),
                                                       in1=place[:, :], op0=ALU.mult, op1=ALU.add))
                dve.wait(scattered[0])
                to_go = chain(lambda e: e.tensor_tensor(scat[:, :], slot_f[:, :], over[:, :], ALU.add))
                yield
                chain(lambda e: e.tensor_scalar(over[:, :], place[:, :], float(CAP - 1), None, ALU.min))
                chain(lambda e, t=t: e.scalar_tensor_tensor(out=slot_of[:, t, :], in0=top_f[:, :], scalar=float(CAP),
                                                            in1=over[:, :], op0=ALU.mult, op1=ALU.add))
                chain(lambda e: e.tensor_scalar(top[:, 0:TOPK], top[:, 0:TOPK], top_sum[:, 0:1], None, ALU.mult))
                chain(lambda e, t=t: e.scalar_tensor_tensor(out=weight_of[:, t, :], in0=place[:, :], scalar=float(CAP),
                                                            in1=top[:, 0:TOPK], op0=ALU.is_lt, op1=ALU.mult))
                pool.wait(to_go, normed, (d["zero"], d["zero"].count))
                for k in range(TOPK):
                    scattered[0] = pool.do(lambda e, k=k: e.indirect_dma_start(
                        disp_hbm, bass.IndirectOffsetOnAxis(scat[:, k:k + 1], 0), x1[:, :], None,
                        bounds_check=E * CAP - 1, oob_is_err=False), scat_counters[0], 16)
                yield

        side_work = []

        def side_step():
            while side_work:
                try:
                    next(side_work[0])
                    return
                except StopIteration:
                    side_work.pop(0)

        pe.wait(once_in)
        pool.wait(once_in)
        load_q(0)
        load_q(1)
        STEPS, LAG = 4, 6
        last = len(groups) * STEPS
        for s in range(last + LAG + 1):
            m, u = divmod(s - LAG, STEPS)
            mv, uv = divmod(s - LAG - 1, STEPS)
            if 0 <= s - LAG < last:
                turned_quad = turn(m, u)
            if s < last:
                scores(s // STEPS, s % STEPS)
                if s % STEPS == STEPS - 1 and s // STEPS + 2 < len(groups):
                    load_q(s // STEPS + 2)
            if 2 <= s < last + 2:
                raise_exp(*divmod(s - 2, STEPS))
            if 0 <= s - LAG < last:
                split_lo(u, *turned_quad)
                if u == 0:
                    invert_sums(m)
                if u == 1:
                    spread_inverse(m)
            if s > LAG:
                times_v(mv, uv)
                if uv == STEPS - 1:
                    finish_group(mv)
                    if groups[mv][1] == H - 1:
                        side_work.append(chunk_end(groups[mv][0]))
            side_step()
        while side_work:
            side_step()
        phase_end()
        for q in (sp, pool, dve):
            q.wait(*((c, c.count) for c in scat_counters))

        sup_in = None
        for a, b in ((sup_w[:, :, :], w_view(w_sup)), (sdown_w[:, :], w_sdown)):
            sup_in = sp.do(lambda e, a=a, b=b: e.dma_start(a, b), d["sup"], 16)
        x1_rows = x1_hbm.rearrange("(g t p) n -> g p t n", t=2, p=P)
        disp_rows = disp_hbm.rearrange("(g t p) n -> g p t n", t=2, p=P)
        y_rows = y_hbm.rearrange("(g t p) n -> g p t n", t=2, p=P)
        items = [("shared", g) for g in range(NT // 2)] + [("expert", e) for e in range(E)]
        rows_in, rows_done, turned_in, up_done, hid_done = {}, {}, {}, {}, {}
        y_stored = [None] * NY
        up_bank, up_free = [pv_acc, misc], [None, None]

        def load_rows(n):
            kind, g = items[n]
            b = n % NB
            if n >= NB:
                sp.wait(*rows_done[n - NB])
            src = x1_rows if kind == "shared" else disp_rows
            rows_in[n] = sp.do(lambda e: e.dma_start(rows[b][:, :, :], src[g]), d[f"r{b}"], 16)
            if kind == "expert":
                sp.do(lambda e: e.dma_start(up_w[b][:, :, :], w_up[g].rearrange("(k p) n -> p k n", p=P)), d[f"r{b}"], 16)
                rows_in[n] = sp.do(lambda e: e.dma_start(down_w[b][:, :], w_down[g]), d[f"r{b}"], 16)

        def flip_rows(n):
            b = n % NB
            i, slot = take_slot()
            view = slot[:, :].rearrange("p (k t q) -> p k t q", k=KC, t=2)
            pe.wait(rows_in[n], *slot_free[i])
            for k in range(KC):
                for t in range(2):
                    made = (lambda e, k=k, t=t: e.transpose(view[:, k, t, :], rows[b][:, t, k * P:(k + 1) * P], ident[:, :]))
                    if (k, t) == (KC - 1, 1):
                        made = pe.do(made, c_pe["turned"])
                    else:
                        pe.do(made)
            rows_done[n] = [made]
            act.wait(made, up_done.get(n - 2))
            turned_in[n] = act.do(lambda e: e.activation(
                rows_t[n % 2][:, :, :], slot[:, :].rearrange("p (k q) -> p k q", k=KC), ACT.Copy), c_act["hi"])
            slot_free[i] = [turned_in[n]]

        def up(n):
            kind, _ = items[n]
            b, o = n % NB, n % 2
            bank = up_bank[o]
            pe.wait(turned_in[n], up_free[o], sup_in)
            rt = rows_t[o]
            if kind == "shared":
                pe.do(bank_product(bank[:, 0:CAP], [(sup_w[:, k, 0:HS], rt[:, k, :]) for k in range(KC)]))
                up_done[n] = made = pe.do(bank_product(bank[:, CAP:2 * CAP], [
                    (sup_w[:, k, HS:2 * HS], rt[:, k, :]) for k in range(KC)]), c_pe["fill"])
                width, gate, value = HS, bank[:, CAP:2 * CAP], bank[:, 0:CAP]
            else:
                up_done[n] = made = pe.do(bank_product(bank[:, 0:CAP], [
                    (up_w[b][:, k, :], rt[:, k, :]) for k in range(KC)]), c_pe["fill"])
                rows_done[n].append(made)
                width, gate, value = HE, bank[0:HE, 0:CAP], bank[HE:2 * HE, 0:CAP]
            act.wait(made, hid_done.get(n - 2))
            raised = act.do(lambda e: e.activation(gate_e[o][0:width, :], gate, ACT.Exp, scale=-1.0), c_act["exp"])
            dve.wait(raised, down_done.get(n - 2))
            chain(lambda e: e.tensor_scalar(gate_e[o][0:width, :], gate_e[o][0:width, :], 1.0, None, ALU.add))
            chain(lambda e: e.reciprocal(gate_e[o][0:width, :], gate_e[o][0:width, :]))
            chain(lambda e: e.tensor_tensor(gate_g[o][0:width, :], gate, gate_e[o][0:width, :], ALU.mult))
            up_free[o] = hid_done[n] = chain(lambda e: e.tensor_tensor(
                hid[o][0:width, :], value, gate_g[o][0:width, :], ALU.mult))

        down_done = {}

        def down(n):
            kind, g = items[n]
            b, o, y = n % NB, n % 2, n % NY
            i, slot = take_slot()
            pe.wait(hid_done[n], *slot_free[i])
            for t in range(2):
                lhs = hid[o][:, t * P:(t + 1) * P] if kind == "shared" else hid[o][0:HE, t * P:(t + 1) * P]
                rhs = sdown_w[:, :] if kind == "shared" else down_w[b][:, :]
                made = pe.do(lambda e, t=t, lhs=lhs, rhs=rhs: e.matmul(
                    slot[:, t * BANK:(t + 1) * BANK], lhs, rhs, start=True, stop=True), c_pe["fill"])
            down_done[n] = made
            rows_done[n].append(made)
            if kind == "shared":
                dve.wait(made)
                added = dve.do(lambda e: e.tensor_tensor(
                    base[:, 2 * g:2 * g + 2, :], slot[:, :].rearrange("p (t n) -> p t n", t=2), rows[b][:, :, :],
                    ALU.add), c_dve["chain"])
                slot_free[i] = [added]
                rows_done[n].append(added)
                return
            dve.wait(made, y_stored[y])
            act.wait(made, y_stored[y])
            left = dve.do(lambda e: e.tensor_copy(y_out[y][:, 0, :], slot[:, 0:BANK]), c_dve["lo"])
            right = act.do(lambda e: e.activation(y_out[y][:, 1, :], slot[:, BANK:2 * BANK], ACT.Copy), c_act["misc"])
            slot_free[i] = [left, right]
            pool.wait(left, right)
            y_stored[y] = pool.do(lambda e: e.dma_start(y_rows[g], y_out[y][:, :, :]), d[f"y{y}"], 16)

        N = len(items)
        AHEAD = NB - 1
        for n in range(AHEAD):
            load_rows(n)
        flip_rows(0)
        flip_rows(1)
        up(0)
        for n in range(N):
            if n + AHEAD < N:
                load_rows(n + AHEAD)
            if n + 2 < N:
                flip_rows(n + 2)
            if n + 1 < N:
                up(n + 1)
            down(n)

        pool.wait(*((d[f"y{b}"], d[f"y{b}"].count) for b in range(NY)))
        got_free, got_in = [None] * NG, {}
        out_tiles = out.rearrange("b (t p) n -> (b t) p n", p=P)

        def gather(t):
            for k in range(TOPK):
                g = (t * TOPK + k) % NG
                pool.wait(got_free[g])
                got_in[t, k] = pool.do(lambda e, g=g, k=k: e.indirect_dma_start(
                    got[g][:, :], None, y_hbm, bass.IndirectOffsetOnAxis(slot_of[:, t, k:k + 1], 0),
                    bounds_check=E * CAP - 1, oob_is_err=False), d_got[g], 16)

        def add_up(t):
            b = t % 2
            for k in range(TOPK):
                g = (t * TOPK + k) % NG
                dve.wait(got_in[t, k])
                got_free[g] = chain(lambda e, g=g, k=k: e.scalar_tensor_tensor(
                    out=base[:, t, :], in0=got[g][:, :], scalar=weight_of[:, t, k:k + 1], in1=base[:, t, :],
                    op0=ALU.mult, op1=ALU.add))
            chain(lambda e: e.bn_stats(f_stats[:, b, :], base[:, t, :]))
            chain(lambda e: e.bn_aggr(f_mv[:, b, :], f_stats[:, b, :]))
            return chain(lambda e: e.tensor_scalar(f_mv[:, b, 1:2], f_mv[:, b, 1:2], EPS, None, ALU.add))

        def store_normed(t, var):
            b = t % 2
            pool.wait(var)
            root = pool_chain(lambda e: e.tensor_tensor(f_rstd[:, b:b + 1], f_mv[:, b, 1:2], half_neg[:, :], ALU.pow))
            dve.wait(root, (d[f"o{b}"], d[f"o{b}"].count))
            normed = chain(lambda e: e.tensor_scalar(
                final[b][:, :], base[:, t, :], f_mv[:, b, 0:1], f_rstd[:, b:b + 1], ALU.subtract, ALU.mult))
            sp.wait(normed)
            sp.do(lambda e: e.dma_start(out_tiles[t], final[b][:, :]), d[f"o{b}"], 16)

        gather(0)
        gather(1)
        var = {}
        for t in range(NT):
            var[t] = add_up(t)
            if t + 2 < NT:
                gather(t + 2)
            if t:
                store_normed(t - 1, var[t - 1])
        store_normed(NT - 1, var[NT - 1])
        sp.wait(*((c, c.count) for c in (*d.values(), *d_got, *scat_counters)))

        block = ctx.enter_context(nc.Block())
        block.sync(sp.run)
        block.gpsimd(pool.run)
        block.scalar(act.run)
        block.vector(dve.run)
        block.tensor(pe.run)


_INS = ["L0_attn_x", "L0_attn_Wq", "L0_attn_bq", "L0_attn_Wk", "L0_attn_bk", "L0_attn_Wv", "L0_attn_bv",
        "L0_attn_Wo", "L0_attn_bo", "L0_ffn_w_gate", "L0_ffn_w_shared_up", "L0_ffn_w_shared_down",
        "L0_ffn_w_up", "L0_ffn_w_down"]
_OUTS = [((1, 2048, 512), "float32")]


def kernel(**inputs):
    import concourse.bacc as _bacc
    from concourse.bass_utils import run_bass_kernel_spmd as _run

    nc = _bacc.Bacc("TRN2", target_bir_lowering=False, num_devices=1)
    arrays, args = {}, []
    for name in _INS:
        a = np.asarray(inputs[name])
        if name in ("L0_attn_bq", "L0_attn_bk"):
            a = a.reshape(-1, P).T
        a = np.ascontiguousarray(a)
        arrays[f"in_{name}"] = a
        args.append(nc.dram_tensor(f"in_{name}", a.shape, mybir.dt.from_np(a.dtype), kind="ExternalInput").ap())
    for i, (shape, dtype) in enumerate(_OUTS):
        dt = mybir.dt.from_np(np.dtype(dtype))
        args.append(nc.dram_tensor(f"out_{i}", shape, dt, kind="ExternalOutput").ap())
    build(nc, *args)
    r = _run(nc, [arrays], core_ids=[0])
    return r.results[0]["out_0"]
```

```python
from contextlib import ExitStack

import numpy as np

import concourse.bass as bass
from concourse import mybir

F32 = mybir.dt.float32
F32R = mybir.dt.float32r
BF16 = mybir.dt.bfloat16
U32 = mybir.dt.uint32
ALU = mybir.AluOpType
ACT = mybir.ActivationFunctionType
AX = mybir.AxisListType

P = 128
BANK = 512


class Counter:

    def __init__(self, handle):
        self.handle, self.count = handle, 0

    def add(self, n):
        self.count += n
        return (self, self.count)


class Queue:

    def __init__(self):
        self.ops, self.seen = [], {}

    def wait(self, *marks):
        for mark in marks:
            if mark is None:
                continue
            counter, value = mark
            if self.seen.get(id(counter), 0) < value:
                self.seen[id(counter)] = value
                self.ops.append(lambda e, h=counter.handle, v=value: e.wait_ge(h, v))

    def do(self, op, counter=None, by=1):
        if counter is None:
            self.ops.append(op)
            return None
        self.ops.append(lambda e, h=counter.handle: op(e).then_inc(h, by))
        return counter.add(by)

    def run(self, e):
        for op in self.ops:
            op(e)


def build(nc, x, Wq, bq, Wk, bk, Wv, bv, Wo, bo, w_gate, w_sup, w_sdown, w_up, w_down, out):
    _, T, C = x.shape
    D = 64
    H = C // D
    SCALE = float(np.sqrt(8.0))
    E = w_gate.shape[1]
    HE = w_down.shape[1]
    HS = w_sdown.shape[0]
    TOPK, CAP, EPS = 6, 256, 1e-5
    KC = C // P
    NT = T // P
    QC = 256
    QT = QC // P
    NCH = T // QC
    HALF = T // 2
    KT4 = T // P // 4
    SKIP = 1 << 17

    ctx = ExitStack()
    with ctx:
        def sb(name, shape, dt=F32, stack=ctx):
            return stack.enter_context(nc.sbuf_tensor(name, shape, dt))

        def counter(name):
            return Counter(ctx.enter_context(nc.semaphore(name)))

        def hbm(name, shape, dt=F32):
            return nc.dram_tensor(name, shape, dt).ap()

        q_hbm = hbm("q_hbm", (H // 2, 2, P, T))
        x1_hbm = hbm("x1_hbm", (T, C))
        disp_hbm = hbm("disp_hbm", (E * CAP, C))
        y_hbm = hbm("y_hbm", (E * CAP, C))

        slots = [ctx.enter_context(nc.psum_tensor(f"slot{i}", [P, 2 * BANK], F32)) for i in range(3)]
        pv_acc = ctx.enter_context(nc.psum_tensor("pv_acc", [P, BANK], F32))
        misc = ctx.enter_context(nc.psum_tensor("misc", [P, BANK], F32))
        slot_free = [[], [], []]
        slot_turn = [0]

        def take_slot():
            i = slot_turn[0] % 3
            slot_turn[0] += 1
            return i, slots[i]

        ident = sb("ident", [P, P])
        slot_of = sb("slot_of", [P, NT, TOPK], U32)
        weight_of = sb("weight_of", [P, NT, TOPK])
        half_neg = sb("half_neg", [P, 1])
        att = ExitStack()
        k_stack = sb("k_stack", [P, H, T], F32R, att)
        v_pair = sb("v_pair", [P, NT, H, P], F32R, att)
        wo_sb = sb("wo_sb", [P, KC, C], F32, att)
        wg_sb = sb("wg_sb", [P, KC, E], F32, att)
        bo_all = sb("bo_all", [P, C], F32, att)
        before = sb("before", [P, P], BF16, att)
        ones_bf = sb("ones_bf", [P, P], BF16, att)
        iota_e = sb("iota_e", [P, E], F32, att)
        count_so_far = sb("count_so_far", [P, E], BF16, att)
        pro = ExitStack()
        x_t = sb("x_t", [P, KC, T], F32, pro)
        w_in = [sb(f"w_in{i}", [P, KC, C], F32, pro) for i in range(2)]
        stage = [sb(f"stage{i}", [P, 2, C], F32, pro) for i in range(2)]
        q_hi = sb("q_hi", [P, 2 * BANK], F32R, pro)
        q_lo = sb("q_lo", [P, 2 * BANK], F32R, pro)
        zeros = sb("zeros", [P, C // 2], F32, pro)
        bias_k = sb("bias_k", [P, KC], F32, pro)
        bias_q = sb("bias_q", [P, KC], F32, pro)
        pro.close()
        prob = sb("prob", [P, 2, QT, T], F32, att)
        p_hi = [sb(f"p_hi{i}", [P, 4, QC], F32R, att) for i in range(2)]
        p_lo = [sb(f"p_lo{i}", [P, 4, QC], F32R, att) for i in range(2)]
        q_stack = [sb(f"q_stack{i}", [P, 2, QC], F32R, att) for i in range(2)]
        row_min = sb("row_min", [P, 2, QT, 2], F32, att)
        row_sum = sb("row_sum", [P, 2, QT, 2], F32, att)
        row_inv = sb("row_inv", [P, QT], F32, att)
        scaled = sb("scaled", [P, QC], F32, att)
        moved = sb("moved", [P, QC], F32, att)
        feats = sb("feats", [P, H // 2, QC], F32, att)
        resid = [sb(f"resid{i}", [P, C], F32, att) for i in range(QT)]
        x1 = sb("x1", [P, C], F32, att)
        x1_t = sb("x1_t", [P, KC, P], F32, att)
        small = sb("small", [P, 20], F32, att)
        stats, top_sum, top_f = small[:, 0:6], small[:, 6:7], small[:, 7:13]
        mean_var, rstd = (small[:, 13:15], small[:, 15:17]), (small[:, 17:18], small[:, 18:19])
        score = sb("score", [P, E], F32, att)
        top = sb("top", [P, 8], F32, att)
        top_i = sb("top_i", [P, 8], U32, att)
        onehot = x1_t[:, 0:TOPK * E // P, :].rearrange("p a b -> p (a b)").rearrange("p (k e) -> p k e", e=E)
        picked = sb("picked", [P, E], BF16, att)
        place, over, slot_f = (x1_t[:, KC - 1, 8 * i:8 * i + TOPK] for i in range(3))
        scat = sb("scat", [P, TOPK], U32, att)
        att.close()
        NB, NY = 5, 3
        rows = [sb(f"rows{i}", [P, 2, C]) for i in range(NB)]
        up_w = [sb(f"up_w{i}", [P, KC, 2 * HE]) for i in range(NB)]
        down_w = [sb(f"down_w{i}", [HE, C]) for i in range(NB)]
        sup_w = sb("sup_w", [P, KC, 2 * HS])
        sdown_w = sb("sdown_w", [HS, C])
        rows_t = [sb(f"rows_t{i}", [P, KC, CAP]) for i in range(2)]
        gate_e = [sb(f"gate_e{i}", [P, CAP]) for i in range(2)]
        gate_g = [sb(f"gate_g{i}", [P, CAP]) for i in range(2)]
        hid = [sb(f"hid{i}", [P, CAP]) for i in range(2)]
        y_out = [sb(f"y_out{i}", [P, 2, C]) for i in range(NY)]
        base = sb("base", [P, NT, C])
        NG = 18
        got = [sb(f"got{i}", [P, C]) for i in range(NG)]
        f_stats = sb("f_stats", [P, 2, 6])
        f_mv = sb("f_mv", [P, 2, 2])
        f_rstd = sb("f_rstd", [P, 2])
        final = [sb(f"final{i}", [P, C]) for i in range(2)]

        pe, act, dve, pool, sp = Queue(), Queue(), Queue(), Queue(), Queue()

        c_pe = {n: counter(f"pe_{n}") for n in ("fill", "scores", "turned", "pv", "misc")}
        c_act = {n: counter(f"act_{n}") for n in ("hi", "exp", "misc")}
        c_dve = {n: counter(f"dve_{n}") for n in ("min", "lo", "chain")}
        c_pool = {n: counter(f"pool_{n}") for n in ("const", "chain", "lo")}
        d = {n: counter(f"dma_{n}") for n in (
            "wk", "wq", "wv", "bias", "bv", "once", "zero", "qst", "moved", "feats", "resid0", "resid1", "sup", "x0", "x1_",
            "q0", "q1", "st", "r0", "r1", "r2", "r3", "r4", "y0", "y1", "y2", "o0", "o1")}
        d_got = [counter(f"dma_got{i}") for i in range(NG)]

        def chain(op):
            dve.wait((c_dve["chain"], c_dve["chain"].count))
            return dve.do(op, c_dve["chain"])

        def pool_chain(op):
            pool.wait((c_pool["chain"], c_pool["chain"].count))
            return pool.do(op, c_pool["chain"])

        def bank_product(dst, pairs, start=True, stop=True):
            for n, (a, b) in enumerate(pairs[:-1]):
                pe.do(lambda e, a=a, b=b, n=n: e.matmul(dst, a, b, start=start and n == 0, stop=False))
            a, b = pairs[-1]
            return lambda e: e.matmul(dst, a, b, start=start and len(pairs) == 1, stop=stop)

        pool.do(lambda e: e.memset(ident[:, :], 0.0), c_pool["const"])
        pool.wait((c_pool["const"], 1))
        ident_ready = pool.do(lambda e: e.affine_select(
            out=ident[:, :], in_=ident[:, :], compare_op=ALU.not_equal, fill=1.0, base=0,
            pattern=[[-1, P]], channel_multiplier=1), c_pool["const"])
        zeros_ready = pool.do(lambda e: e.memset(zeros[:, :], 0.0), c_pool["const"])
        pool.do(lambda e: e.memset(half_neg[:, :], -0.5))
        pool.do(lambda e: e.memset(count_so_far[:, :], 0.0))
        pool.do(lambda e: e.iota(iota_e[:, :], [[1, E]], base=0, channel_multiplier=0,
                                 allow_small_or_imprecise_dtypes=True))
        ones_ready = pool.do(lambda e: e.memset(ones_bf[:, :], 1.0), c_pool["const"])
        pool.wait(ones_ready)
        consts = pool.do(lambda e: e.affine_select(
            out=before[:, :], in_=ones_bf[:, :], compare_op=ALU.is_gt, fill=0.0, base=0,
            pattern=[[1, P]], channel_multiplier=-1), c_pool["const"])

        def w_view(w):
            return w.rearrange("(k p) n -> p k n", p=P)

        x_rows = x.rearrange("b (g t p) n -> (b g) p t n", t=2, p=P)
        x_landed, x_read = [None] * (NT // 2), [None] * 2
        for g in range(2):
            x_landed[g] = sp.do(lambda e, g=g: e.dma_start(stage[g][:, :, :], x_rows[g]), d[("x0", "x1_")[g]], 16)
        wk_in = sp.do(lambda e: e.dma_start(w_in[0][:, :, :], w_view(Wk)), d["wk"], 16)
        for b, t in ((bk, bias_k), (bq, bias_q)):
            bias_in = sp.do(lambda e, b=b, t=t: e.dma_start(t[:, :], b), d["bias"], 16)
        wq_in = sp.do(lambda e: e.dma_start(w_in[1][:, :, :], w_view(Wq)), d["wq"], 16)

        turned = None
        for g in range(NT // 2):
            if g >= 2:
                sp.wait(x_read[g % 2])
                x_landed[g] = sp.do(lambda e, g=g: e.dma_start(stage[g % 2][:, :, :], x_rows[g]),
                                    d[("x0", "x1_")[g % 2]], 16)
            i, slot = take_slot()
            view = slot[:, :].rearrange("p (t k q) -> p t k q", t=2, k=KC)
            pe.wait(ident_ready, x_landed[g], *slot_free[i])
            for t in range(2):
                for k in range(KC):
                    last = (lambda e, g=g, t=t, k=k, view=view: e.transpose(
                        view[:, t, k, :], stage[g % 2][:, t, k * P:(k + 1) * P], ident[:, :]))
                    if (t, k) == (1, KC - 1):
                        x_read[g % 2] = pe.do(last, c_pe["fill"])
                    else:
                        pe.do(last)
            dst = x_t[:, :, g * 2 * P:(g + 1) * 2 * P].rearrange("p k (t q) -> p k t q", t=2)
            src = slot[:, :].rearrange("p (t k q) -> p k t q", t=2, k=KC)
            if g % 2:
                act.wait(x_read[g % 2])
                for k in range(KC):
                    turned_a = act.do(lambda e, dst=dst, src=src, k=k: e.activation(dst[:, k], src[:, k], ACT.Copy),
                                      c_act["misc"])
                slot_free[i] = [turned_a]
            else:
                dve.wait(x_read[g % 2])
                turned_d = dve.do(lambda e, dst=dst, src=src: e.tensor_copy(dst, src), c_dve["chain"])
                slot_free[i] = [turned_d]

        sp.wait(zeros_ready)
        zero_row = zeros[:, :].unsqueeze(1).to_broadcast([P, 4, C // 2])
        disp_pieces = disp_hbm.rearrange("(g p t) (u n) -> g p (t u) n", p=P, t=2, u=2)
        zero_pieces = [lambda e, g=g: e.dma_start(disp_pieces[g], zero_row) for g in range(E * CAP // (P * 2))]

        def zero_some(count):
            for _ in range(count):
                if zero_pieces:
                    sp.do(zero_pieces.pop(0), d["zero"], 16)

        q_stored = None
        for name, w, w_landed, bias in (("k", w_in[0], wk_in, bias_k), ("q", w_in[1], wq_in, bias_q)):
            for pair in range(H // 2):
                for g in range(T // (2 * BANK)):
                    tok = slice(g * 2 * BANK, (g + 1) * 2 * BANK)
                    i, slot = take_slot()
                    pe.wait(w_landed, turned_a, turned_d, *slot_free[i])
                    for n in range(2):
                        cols = slice(g * 2 * BANK + n * BANK, g * 2 * BANK + (n + 1) * BANK)
                        last = bank_product(slot[:, n * BANK:(n + 1) * BANK], [
                            (w[:, k, pair * P:(pair + 1) * P], x_t[:, k, cols]) for k in range(KC)])
                        made = pe.do(last, c_pe["fill"])
                    if name == "k":
                        zero_some(4)
                        for odd in range(2):
                            h, hi, lo = 2 * pair + odd, slice(odd * D, (odd + 1) * D), slice((1 - odd) * D, (2 - odd) * D)
                            act.wait(made, bias_in)
                            rounded = act.do(lambda e, h=h, hi=hi, slot=slot, tok=tok, bias=bias, pair=pair: e.activation(
                                k_stack[hi, h, tok], slot[hi, :], ACT.Identity, bias=bias[hi, pair:pair + 1]), c_act["hi"])
                            dve.wait(rounded)
                            slot_free[i] = [dve.do(lambda e, h=h, hi=hi, lo=lo, slot=slot, tok=tok, bias=bias, pair=pair:
                                                  e.scalar_tensor_tensor(
                                out=k_stack[lo, h, tok], in0=slot[hi, :], scalar=bias[hi, pair:pair + 1],
                                in1=k_stack[hi, h, tok].bitcast(F32), op0=ALU.add, op1=ALU.subtract), c_dve["lo"])]
                    else:
                        act.wait(made, bias_in, q_stored)
                        rounded = act.do(lambda e, slot=slot, bias=bias, pair=pair: e.activation(
                            q_hi[:, :], slot[:, :], ACT.Identity, bias=bias[:, pair:pair + 1]), c_act["hi"])
                        dve.wait(rounded)
                        slot_free[i] = [dve.do(lambda e, slot=slot, bias=bias, pair=pair: e.scalar_tensor_tensor(
                            out=q_lo[:, :], in0=slot[:, :], scalar=bias[:, pair:pair + 1],
                            in1=q_hi[:, :].bitcast(F32), op0=ALU.add, op1=ALU.subtract), c_dve["lo"])]
                        sp.wait(*slot_free[i])
                        for part, src in ((0, q_hi), (1, q_lo)):
                            q_stored = sp.do(lambda e, src=src, part=part, pair=pair, tok=tok: e.dma_start(
                                q_hbm[pair, part, :, tok], src[:, :].bitcast(F32)), d["qst"], 16)
            if name == "k":
                sp.wait(made)
                wv_in = sp.do(lambda e: e.dma_start(w_in[0][:, :, :], w_view(Wv)), d["wv"], 16)
                bv_all = stage[0][:, 0, :]
                bv_in = sp.do(lambda e: e.dma_start(bv_all, bv.partition_broadcast(P)), d["bv"], 16)
                for a, b in ((wo_sb[:, :, :], w_view(Wo)), (wg_sb[:, :, :], w_view(w_gate)),
                             (bo_all[:, :], bo.partition_broadcast(P))):
                    once_in = sp.do(lambda e, a=a, b=b: e.dma_start(a, b), d["once"], 16)

        v_plain = stage[1]
        for g in range(NT // 2):
            zero_some(4)
            i, slot = take_slot()
            pe.wait(wv_in, *slot_free[i])
            for t in range(2):
                last = bank_product(slot[:, t * BANK:(t + 1) * BANK], [
                    (x_t[:, k, (2 * g + t) * P:(2 * g + t + 1) * P], w_in[0][:, k, :]) for k in range(KC)])
                made = pe.do(last, c_pe["fill"])
            dve.wait(made, bv_in, (c_pool["chain"], c_pool["chain"].count), (c_act["hi"], c_act["hi"].count))
            added = dve.do(lambda e, slot=slot: e.tensor_tensor(
                v_plain[:, :, :], slot[:, :].rearrange("p (t n) -> p t n", t=2),
                bv_all.unsqueeze(1).to_broadcast([P, 2, C]), ALU.add), c_dve["chain"])
            slot_free[i] = [added]
            act.wait(added)
            for t in range(2):
                src = v_plain[:, t, :].rearrange("p (h c) -> p h c", h=H)
                rounded = act.do(lambda e, g=g, t=t, src=src: e.activation(
                    v_pair[:, 2 * g + t, :, 0:D], src, ACT.Copy), c_act["hi"])
            pool.wait(rounded)
            for t in range(2):
                src = v_plain[:, t, :].rearrange("p (h c) -> p h c", h=H)
                v_made = pool_chain(lambda e, g=g, t=t, src=src: e.tensor_tensor(
                    v_pair[:, 2 * g + t, :, D:P], src, v_pair[:, 2 * g + t, :, 0:D].bitcast(F32), ALU.subtract))

        def phase_end():
            marks = [(c, c.count) for c in (*c_pe.values(), *c_act.values(), *c_dve.values(), *c_pool.values(),
                                            *d.values()) if c.count]
            for q in (pe, act, dve, pool, sp):
                q.wait(*marks)

        phase_end()

        groups = [(c, h) for c in range(NCH) for h in range(H)]
        q_in, q_read = {}, [None] * 2
        lowest, exp_done, t_read, hi_done, lo_done, pv_read = {}, {}, {}, {}, {}, [None] * 2
        copy_read = {}
        misc_free = [None]
        pv_free = [None]

        def load_q(m):
            c, h = groups[m]
            sp.wait(q_read[m % 2])
            src = q_hbm[h // 2, :, (h % 2) * D:(h % 2 + 1) * D, c * QC:(c + 1) * QC].rearrange("s c q -> c s q")
            for half in (slice(0, D), slice(D, P)):
                q_in[m] = sp.do(lambda e, half=half: e.dma_start(q_stack[m % 2][half, :, :].bitcast(F32), src),
                                d[f"q{m % 2}"], 16)

        def scores(m, u):
            c, h = groups[m]
            half, j = divmod(u, QT)
            i, slot = take_slot()
            pe.wait(q_in[m])
            qs = q_stack[m % 2]
            for n in range(2):
                pe.wait(*slot_free[i][:n + 1])
                for part in range(2):
                    keys = slice(half * HALF + n * BANK, half * HALF + (n + 1) * BANK)
                    op = (lambda e, part=part, n=n, keys=keys: e.matmul(
                        slot[:, n * BANK:(n + 1) * BANK], qs[:, part, j * P:(j + 1) * P], k_stack[:, h, keys],
                        start=part == 0, stop=part == 1))
                    if (n, part) == (1, 1):
                        made = pe.do(op, c_pe["scores"])
                    else:
                        pe.do(op)
            q_read[m % 2] = made
            return i, slot, made

        def keep_scores(m, u, i, slot, made):
            half, j = divmod(u, QT)
            dve.wait(made, t_read.get((m - 2, half)), copy_read.get((m - 2, half)))
            first = 3.0e38 if half == 0 else row_min[:, m % 2, j, 0:1]
            if half:
                dve.wait((c_dve["min"], c_dve["min"].count))
            low = dve.do(lambda e: e.tensor_scalar(
                prob[:, m % 2, j, half * HALF:(half + 1) * HALF], slot[:, :], -1.0 / SCALE, first, ALU.mult, ALU.min,
                accum_out=row_min[:, m % 2, j, half:half + 1]), c_dve["min"])
            slot_free[i] = [low]
            lowest[m, j] = low

        def raise_exp(m, u):
            half, j = divmod(u, QT)
            act.wait(lowest[m, j])
            exp_done[m, j, half] = act.do(lambda e: e.activation(
                prob[:, m % 2, j, half * HALF:(half + 1) * HALF], prob[:, m % 2, j, half * HALF:(half + 1) * HALF],
                ACT.Exp, bias=row_min[:, m % 2, j, 1:2], scale=-1.0,
                accum_out=row_sum[:, m % 2, j, half:half + 1]), c_act["exp"])

        def turn(m, u):
            i, slot = take_slot()
            view = slot[:, :].rearrange("p (t q) -> p t q", t=4)
            pe.wait(*slot_free[i], *(exp_done[m, j, u // 2] for j in range(QT)))
            b = u % 2
            for t in range(4):
                for j in range(QT):
                    op = (lambda e, t=t, j=j: e.transpose(
                        view[:, t, j * P:(j + 1) * P], prob[:, m % 2, j, (4 * u + t) * P:(4 * u + t + 1) * P],
                        ident[:, :]))
                    if (t % 2, j) == (1, QT - 1):
                        made = pe.do(op, c_pe["turned"])
                    else:
                        pe.do(op)
                if t % 2:
                    two = slice(t - 1, t + 1)
                    act.wait(made, pv_read[b])
                    hi_done[b, t // 2] = act.do(lambda e, two=two: e.activation(
                        p_hi[b][:, two, :], view[:, two, :], ACT.Copy), c_act["hi"])
            if u % 2:
                copy = prob[:, m % 2, :, (4 * u + 2) * P:(4 * u + 4) * P]
                copied = act.do(lambda e, two=two: e.activation(copy, view[:, two, :], ACT.Copy), c_act["misc"])
                slot_free[i] = [copied]
                pool.wait(copied)
                lo_done[b, 1] = copy_read[m, u // 2] = pool.do(lambda e, two=two: e.tensor_tensor(
                    p_lo[b][:, two, :], copy, p_hi[b][:, two, :].bitcast(F32), ALU.subtract), c_pool["lo"])
            t_read[m, u // 2] = made
            return i, view

        def split_lo(u, i, view):
            b = u % 2
            for half in range(2 - u % 2):
                dve.wait(hi_done[b, half])
                two = slice(2 * half, 2 * half + 2)
                lo_done[b, half] = dve.do(lambda e, two=two: e.tensor_tensor(
                    p_lo[b][:, two, :], view[:, two, :], p_hi[b][:, two, :].bitcast(F32), ALU.subtract), c_dve["lo"])
            slot_free[i] = [lo_done[b, 0], slot_free[i][0] if u % 2 else lo_done[b, 1]]

        def times_v(m, u):
            c, h = groups[m]
            b = u % 2
            if u == 0:
                pe.wait(pv_free[0])
            for t in range(4):
                pe.wait(hi_done[b, t // 2], lo_done[b, t // 2])
                for part, src in enumerate((p_hi[b], p_lo[b])):
                    kt = 4 * u + t
                    op = (lambda e, kt=kt, t=t, part=part, src=src: e.matmul(
                        pv_acc[:, 0:QC], v_pair[:, kt, h, :], src[:, t, :], start=kt == 0 and part == 0,
                        stop=kt == NT - 1 and part == 1))
                    if (t, part) == (3, 1):
                        pv_read[b] = pe.do(op, c_pe["pv"])
                    else:
                        pe.do(op)

        inv_done = {}

        inverted = {}

        def invert_sums(m):
            dve.wait(*(exp_done[m, j, 1] for j in range(QT)))
            chain(lambda e: e.tensor_tensor(row_inv[:, :], row_sum[:, m % 2, :, 0], row_sum[:, m % 2, :, 1], ALU.add))
            inverted[m] = chain(lambda e: e.reciprocal(row_inv[:, :], row_inv[:, :]))

        def spread_inverse(m):
            pe.wait(inverted[m], misc_free[0])
            for j in range(QT):
                made = pe.do(lambda e, j=j: e.transpose(
                    misc[:, j * P:(j + 1) * P], row_inv[:, j:j + 1].to_broadcast([P, P]), ident[:, :]), c_pe["misc"])
            act.wait(made, feats_done.get(m - 1))
            inv_done[m] = act.do(lambda e: e.activation(scaled[:, :], misc[:, 0:QC], ACT.Copy), c_act["misc"])
            misc_free[0] = inv_done[m]

        feats_read, feats_done, moved_done = [None], {}, [None]

        def finish_group(m):
            dve.wait(inv_done[m], pv_read[1], moved_done[0])
            pv_free[0] = done = dve.do(lambda e: e.tensor_tensor(
                scaled[:, :], pv_acc[:, 0:QC], scaled[:, :], ALU.mult), c_dve["chain"])
            sp.wait(done)
            return done, sp.do(lambda e: e.dma_start(moved[0:D, :], scaled[D:P, :]), d["moved"], 16)

        def join_halves(m, done, lo_in):
            pair, odd = divmod(groups[m][1], 2)
            target = moved[0:D, :] if odd else feats[0:D, pair, :]
            pool.wait(done, lo_in, feats_read[0])
            moved_done[0] = feats_done[m] = pool_chain(lambda e: e.tensor_tensor(
                target, scaled[0:D, :], moved[0:D, :], ALU.add))
            if odd:
                sp.wait(feats_done[m])
                moved_done[0] = feats_done[m] = sp.do(lambda e: e.dma_start(
                    feats[D:P, pair, :], target), d["feats"], 16)

        x_tiles = x.rearrange("b (t p) n -> (b t) p n", p=P)
        x1_stored, scattered, counted = [None], [None], [None]
        scat_counters = [counter("dma_scat")]
        resid_free = [None] * QT

        resid_in, biased = {}, {}

        def load_resid(c):
            for j in range(QT):
                sp.wait(resid_free[j])
                resid_in[j] = sp.do(lambda e, j=j: e.dma_start(resid[j][:, :], x_tiles[c * QT + j]), d[f"resid{j}"], 16)

        def bias_resid(j):
            pool.wait(resid_in[j])
            biased[j] = pool_chain(lambda e: e.tensor_tensor(resid[j][:, :], resid[j][:, :], bo_all[:, :], ALU.add))

        def chunk_end(c):
            def steps(count):
                yield from [None] * (2 * count)

            def project(j):
                pe.wait(feats_done[c * H + H - 1], feats_done[c * H + H - 2], misc_free[0])
                made = pe.do(bank_product(misc[:, :], [
                    (feats[:, k, j * P:(j + 1) * P], wo_sb[:, k, :]) for k in range(KC)]), c_pe["misc"])
                feats_read[0] = made
                return made

            def add_resid(j, made):
                dve.wait(made, biased[j])
                misc_free[0] = chain(lambda e: e.tensor_tensor(resid[j][:, :], misc[:, :], resid[j][:, :], ALU.add))

            def measure(j):
                chain(lambda e: e.bn_stats(stats[:, :], resid[j][:, :]))
                chain(lambda e: e.bn_aggr(mean_var[j][:, :], stats[:, :]))
                return chain(lambda e: e.tensor_scalar(mean_var[j][:, 1:2], mean_var[j][:, 1:2], EPS, None, ALU.add))

            def root(j, var):
                pool.wait(var)
                return pool_chain(lambda e: e.tensor_tensor(rstd[j][:, :], mean_var[j][:, 1:2], half_neg[:, :], ALU.pow))

            def dispatch(t, j, rooted):
                dve.wait(rooted, scattered[0], x1_stored[0])
                normed = resid_free[j] = chain(lambda e: e.tensor_scalar(
                    x1[:, :], resid[j][:, :], mean_var[j][:, 0:1], rstd[j][:, 0:1], ALU.subtract, ALU.mult))
                sp.wait(normed)
                x1_stored[0] = sp.do(lambda e: e.dma_start(x1_hbm[t * P:(t + 1) * P, :], x1[:, :]), d["st"], 16)
                yield
                pe.wait(normed, misc_free[0])
                for k in range(KC):
                    made = pe.do(lambda e, k=k: e.transpose(
                        misc[:, k * P:(k + 1) * P], x1[:, k * P:(k + 1) * P], ident[:, :]), c_pe["misc"])
                yield
                act.wait(made, (c_dve["chain"], c_dve["chain"].count))
                misc_free[0] = flipped = act.do(lambda e: e.activation(
                    x1_t[:, :, :], misc[:, :].rearrange("p (k q) -> p k q", k=KC), ACT.Copy), c_act["misc"])
                yield
                pe.wait(flipped, misc_free[0])
                gated = made = pe.do(bank_product(misc[:, 0:E], [(x1_t[:, k, :], wg_sb[:, k, :]) for k in range(KC)]),
                                     c_pe["misc"])
                yield
                act.wait(made, (c_dve["chain"], c_dve["chain"].count))
                misc_free[0] = raised = act.do(lambda e: e.activation(score[:, :], misc[:, 0:E], ACT.Exp, scale=-1.0),
                                               c_act["misc"])
                yield from steps(1)
                dve.wait(raised)
                chain(lambda e: e.tensor_scalar(score[:, :], score[:, :], 1.0, None, ALU.add))
                chain(lambda e: e.reciprocal(score[:, :], score[:, :]))
                yield from steps(1)
                chain(lambda e: e.max(top[:, :], score[:, :]))
                chain(lambda e: e.max_index(top_i[:, :], top[:, :], score[:, :]))
                chain(lambda e: e.tensor_copy(top_f[:, :], top_i[:, 0:TOPK]))
                yield from steps(1)
                dve.wait(gated)
                chain(lambda e: e.tensor_tensor(
                    onehot[:, :, :], iota_e[:, :].unsqueeze(1).to_broadcast([P, TOPK, E]),
                    top_f[:, :].unsqueeze(2).to_broadcast([P, TOPK, E]), ALU.is_equal))
                yield from steps(1)
                dve.wait(counted[0])
                mask = chain(lambda e: e.tensor_reduce(
                    picked[:, :], onehot[:, :, :].rearrange("p k e -> p e k"), AX.X, ALU.max))
                yield
                pe.wait(mask, misc_free[0], counted[0])
                made = pe.do(bank_product(misc[:, 0:E], [
                    (before[:, :], picked[:, :]), (ones_bf[:, :], count_so_far[:, :])]), c_pe["misc"])
                yield
                pool.wait(made, mask)
                counted[0] = pool_chain(lambda e: e.tensor_tensor(
                    count_so_far[:, :], count_so_far[:, :], picked[:, :], ALU.add))
                dve.wait(made)
                misc_free[0] = chain(lambda e: e.tensor_tensor(
                    onehot[:, :, :], onehot[:, :, :], misc[:, 0:E].unsqueeze(1).to_broadcast([P, TOPK, E]), ALU.mult))
                yield from steps(1)
                chain(lambda e: e.tensor_reduce(place[:, :], onehot[:, :, :], AX.X, ALU.add))
                yield from steps(1)
                chain(lambda e: e.tensor_scalar(over[:, :], place[:, :], float(CAP), float(SKIP), ALU.is_ge, ALU.mult))
                chain(lambda e: e.scalar_tensor_tensor(out=slot_f[:, :], in0=top_f[:, :], scalar=float(CAP),
                                                       in1=place[:, :], op0=ALU.mult, op1=ALU.add))
                to_go = chain(lambda e: e.tensor_tensor(scat[:, :], slot_f[:, :], over[:, :], ALU.add))
                pool.wait(to_go, normed, (d["zero"], d["zero"].count))
                for k in range(TOPK):
                    scattered[0] = pool.do(lambda e, k=k: e.indirect_dma_start(
                        disp_hbm, bass.IndirectOffsetOnAxis(scat[:, k:k + 1], 0), x1[:, :], None,
                        bounds_check=E * CAP - 1, oob_is_err=False), scat_counters[0], 16)
                    if k == 1:
                        chain(lambda e: e.tensor_scalar(over[:, :], place[:, :], float(CAP - 1), None, ALU.min))
                        chain(lambda e: e.scalar_tensor_tensor(
                            out=slot_of[:, t, :], in0=top_f[:, :], scalar=float(CAP), in1=over[:, :],
                            op0=ALU.mult, op1=ALU.add))
                        chain(lambda e: e.tensor_reduce(top_sum[:, :], top[:, 0:TOPK], AX.X, ALU.add))
                    if k == 3:
                        chain(lambda e: e.reciprocal(top_sum[:, :], top_sum[:, :]))
                        chain(lambda e: e.tensor_scalar(top[:, 0:TOPK], top[:, 0:TOPK], top_sum[:, 0:1], None, ALU.mult))
                        chain(lambda e: e.scalar_tensor_tensor(
                            out=weight_of[:, t, :], in0=place[:, :], scalar=float(CAP), in1=top[:, 0:TOPK],
                            op0=ALU.is_lt, op1=ALU.mult))
                    if k % 2:
                        yield from steps(1)

            yield from steps(2)
            yield
            made = project(0)
            yield
            add_resid(0, made)
            yield from steps(1)
            var = measure(0)
            yield
            made = project(1)
            yield
            add_resid(1, made)
            rooted = root(0, var)
            yield from steps(1)
            rooted, rooted_1 = rooted, root(1, measure(1))
            yield from dispatch(c * QT, 0, rooted)
            yield from steps(1)
            yield from dispatch(c * QT + 1, 1, rooted_1)

        side_work = []

        def side_step():
            while side_work:
                try:
                    next(side_work[0])
                    return
                except StopIteration:
                    side_work.pop(0)

        pe.wait(once_in)
        pool.wait(once_in)
        load_q(0)
        load_q(1)
        STEPS, LAG = 4, 6
        later = []
        last = len(groups) * STEPS
        for s in range(last + LAG + 2):
            m, u = divmod(s - LAG, STEPS)
            mv, uv = divmod(s - LAG - 1, STEPS)
            if 0 <= s - LAG < last:
                turned_quad = turn(m, u)
            if s < last:
                made_scores = scores(s // STEPS, s % STEPS)
                if s % STEPS == STEPS - 1 and s // STEPS + 2 < len(groups):
                    load_q(s // STEPS + 2)
            side_step()
            if 0 <= s - LAG < last:
                split_lo(u, *turned_quad)
            if LAG < s <= last + LAG:
                times_v(mv, uv)
                if uv == STEPS - 1:
                    later.append((s + 1, lambda mv=mv, halves=finish_group(mv): join_halves(mv, *halves)))
                    chunk, head = groups[mv]
                    if head == H - 3:
                        load_resid(chunk)
                        later.append((s + 2, lambda: bias_resid(0)))
                        later.append((s + 4, lambda: bias_resid(1)))
                    if head == H - 1:
                        side_work.append(chunk_end(chunk))
            if s < last:
                keep_scores(s // STEPS, s % STEPS, *made_scores)
            if 3 <= s < last + 3:
                raise_exp(*divmod(s - 3, STEPS))
            if 0 <= s - LAG < last and u == 1:
                invert_sums(m)
            for due, step in [x for x in later if x[0] == s]:
                step()
            side_step()
            if 0 <= s - LAG < last and u == 2:
                spread_inverse(m)
        phase_end()

        sup_in = None
        for a, b in ((sup_w[:, :, :], w_view(w_sup)), (sdown_w[:, :], w_sdown)):
            sup_in = sp.do(lambda e, a=a, b=b: e.dma_start(a, b), d["sup"], 16)
        x1_rows = x1_hbm.rearrange("(g t p) n -> g p t n", t=2, p=P)
        disp_rows = disp_hbm.rearrange("(g t p) n -> g p t n", t=2, p=P)
        y_rows = y_hbm.rearrange("(g t p) n -> g p t n", t=2, p=P)
        items = [("shared", g) for g in range(NT // 2)] + [("expert", e) for e in range(E)]
        rows_in, rows_done, turned_in, up_done, hid_done = {}, {}, {}, {}, {}
        y_stored = [None] * NY
        up_bank, up_free = [pv_acc, misc], [pv_free[0], None]

        def load_rows(n):
            kind, g = items[n]
            b = n % NB
            if n >= NB:
                sp.wait(*rows_done[n - NB])
            src = x1_rows if kind == "shared" else disp_rows
            if kind == "expert":
                sp.do(lambda e: e.dma_start(up_w[b][:, :, :], w_up[g].rearrange("(k p) n -> p k n", p=P)), d[f"r{b}"], 16)
                sp.do(lambda e: e.dma_start(down_w[b][:, :], w_down[g]), d[f"r{b}"], 16)
                sp.wait(scattered[0])
            else:
                sp.wait(x1_stored[0])
            rows_in[n] = sp.do(lambda e: e.dma_start(rows[b][:, :, :], src[g]), d[f"r{b}"], 16)

        def flip_rows(n):
            b = n % NB
            i, slot = take_slot()
            view = slot[:, :].rearrange("p (k t q) -> p k t q", k=KC, t=2)
            pe.wait(rows_in[n], *slot_free[i])
            for k in range(KC):
                for t in range(2):
                    made = (lambda e, k=k, t=t: e.transpose(view[:, k, t, :], rows[b][:, t, k * P:(k + 1) * P], ident[:, :]))
                    if (k, t) == (KC - 1, 1):
                        made = pe.do(made, c_pe["turned"])
                    else:
                        pe.do(made)
            rows_done[n] = [made]
            act.wait(made, up_done.get(n - 2))
            turned_in[n] = act.do(lambda e: e.activation(
                rows_t[n % 2][:, :, :], slot[:, :].rearrange("p (k q) -> p k q", k=KC), ACT.Copy), c_act["hi"])
            slot_free[i] = [turned_in[n]]

        def up(n):
            kind, _ = items[n]
            b, o = n % NB, n % 2
            pe.wait(turned_in[n], sup_in)
            rt = rows_t[o]
            if kind == "shared":
                i, bank = take_slot()
                pe.wait(*slot_free[i])
                pe.do(bank_product(bank[:, 0:CAP], [(sup_w[:, k, 0:HS], rt[:, k, :]) for k in range(KC)]))
                up_done[n] = made = pe.do(bank_product(bank[:, CAP:2 * CAP], [
                    (sup_w[:, k, HS:2 * HS], rt[:, k, :]) for k in range(KC)]), c_pe["fill"])
                width, gate, value = HS, bank[:, CAP:2 * CAP], bank[:, 0:CAP]
            else:
                bank = up_bank[o]
                pe.wait(up_free[o])
                up_done[n] = made = pe.do(bank_product(bank[:, 0:CAP], [
                    (up_w[b][:, k, :], rt[:, k, :]) for k in range(KC)]), c_pe["fill"])
                rows_done[n].append(made)
                width, gate, value = HE, bank[0:HE, 0:CAP], bank[HE:2 * HE, 0:CAP]
            act.wait(made, hid_done.get(n - 2))
            bent = act.do(lambda e: e.activation(gate_e[o][0:width, :], gate, ACT.Tanh, scale=0.5), c_act["exp"])
            dve.wait(bent, down_done.get(n - 2))
            chain(lambda e: e.scalar_tensor_tensor(out=gate_g[o][0:width, :], in0=gate_e[o][0:width, :], scalar=1.0,
                                                   in1=gate, op0=ALU.add, op1=ALU.mult))
            hid_done[n] = chain(lambda e: e.scalar_tensor_tensor(
                out=hid[o][0:width, :], in0=gate_g[o][0:width, :], scalar=0.5, in1=value, op0=ALU.mult, op1=ALU.mult))
            if kind == "shared":
                slot_free[i] = [hid_done[n]]
            else:
                up_free[o] = hid_done[n]

        down_done = {}

        def down(n):
            kind, g = items[n]
            b, o, y = n % NB, n % 2, n % NY
            i, slot = take_slot()
            pe.wait(hid_done[n], *slot_free[i])
            for t in range(2):
                lhs = hid[o][:, t * P:(t + 1) * P] if kind == "shared" else hid[o][0:HE, t * P:(t + 1) * P]
                rhs = sdown_w[:, :] if kind == "shared" else down_w[b][:, :]
                made = pe.do(lambda e, t=t, lhs=lhs, rhs=rhs: e.matmul(
                    slot[:, t * BANK:(t + 1) * BANK], lhs, rhs, start=True, stop=True), c_pe["fill"])
            down_done[n] = made
            rows_done[n].append(made)
            if kind == "shared":
                dve.wait(made)
                added = dve.do(lambda e: e.tensor_tensor(
                    base[:, 2 * g:2 * g + 2, :], slot[:, :].rearrange("p (t n) -> p t n", t=2), rows[b][:, :, :],
                    ALU.add), c_dve["chain"])
                slot_free[i] = [added]
                rows_done[n].append(added)
                return
            dve.wait(made, y_stored[y])
            act.wait(made, y_stored[y])
            left = dve.do(lambda e: e.tensor_copy(y_out[y][:, 0, :], slot[:, 0:BANK]), c_dve["lo"])
            right = act.do(lambda e: e.activation(y_out[y][:, 1, :], slot[:, BANK:2 * BANK], ACT.Copy), c_act["misc"])
            slot_free[i] = [left, right]
            pool.wait(left, right)
            y_stored[y] = pool.do(lambda e: e.dma_start(y_rows[g], y_out[y][:, :, :]), d[f"y{y}"], 16)

        N = len(items)
        AHEAD, SIDE = NB - 1, 4
        CLEAR = NCH - 1

        def beside(count):
            for _ in range(count):
                side_step()

        loaded = 0
        for n in range(-2, N):
            if n + 2 == CLEAR:
                while side_work:
                    side_step()
                up_free[1] = misc_free[0]
            while loaded < N and loaded <= n + AHEAD and (loaded < CLEAR or n + 2 >= CLEAR):
                load_rows(loaded)
                loaded += 1
            if n + 2 < N:
                flip_rows(n + 2)
            beside(SIDE)
            if 0 <= n + 1 < N:
                up(n + 1)
            beside(SIDE)
            if n >= 0:
                down(n)
            beside(SIDE)

        pool.wait(*((d[f"y{b}"], d[f"y{b}"].count) for b in range(NY)))
        pool.wait(*((c, c.count) for c in (*c_pe.values(), *c_act.values(), *c_dve.values(), *c_pool.values())))
        got_free, got_in = [None] * NG, {}
        out_tiles = out.rearrange("b (t p) n -> (b t) p n", p=P)

        def gather(t):
            for k in range(TOPK):
                g = (t * TOPK + k) % NG
                pool.wait(got_free[g])
                got_in[t, k] = pool.do(lambda e, g=g, k=k: e.indirect_dma_start(
                    got[g][:, :], None, y_hbm, bass.IndirectOffsetOnAxis(slot_of[:, t, k:k + 1], 0),
                    bounds_check=E * CAP - 1, oob_is_err=False), d_got[g], 16)

        def add_up(t):
            b = t % 2
            for k in range(TOPK):
                g = (t * TOPK + k) % NG
                dve.wait(got_in[t, k])
                got_free[g] = chain(lambda e, g=g, k=k: e.scalar_tensor_tensor(
                    out=base[:, t, :], in0=got[g][:, :], scalar=weight_of[:, t, k:k + 1], in1=base[:, t, :],
                    op0=ALU.mult, op1=ALU.add))
            chain(lambda e: e.bn_stats(f_stats[:, b, :], base[:, t, :]))
            chain(lambda e: e.bn_aggr(f_mv[:, b, :], f_stats[:, b, :]))
            return chain(lambda e: e.tensor_scalar(f_mv[:, b, 1:2], f_mv[:, b, 1:2], EPS, None, ALU.add))

        def store_normed(t, var):
            b = t % 2
            pool.wait(var)
            root = pool_chain(lambda e: e.tensor_tensor(f_rstd[:, b:b + 1], f_mv[:, b, 1:2], half_neg[:, :], ALU.pow))
            dve.wait(root, (d[f"o{b}"], d[f"o{b}"].count))
            normed = chain(lambda e: e.tensor_scalar(
                final[b][:, :], base[:, t, :], f_mv[:, b, 0:1], f_rstd[:, b:b + 1], ALU.subtract, ALU.mult))
            sp.wait(normed)
            sp.do(lambda e: e.dma_start(out_tiles[t], final[b][:, :]), d[f"o{b}"], 16)

        gather(0)
        gather(1)
        var = {}
        for t in range(NT):
            var[t] = add_up(t)
            if t + 2 < NT:
                gather(t + 2)
            if t:
                store_normed(t - 1, var[t - 1])
        store_normed(NT - 1, var[NT - 1])
        sp.wait(*((c, c.count) for c in (*d.values(), *d_got, *scat_counters)))

        block = ctx.enter_context(nc.Block())
        block.sync(sp.run)
        block.gpsimd(pool.run)
        block.scalar(act.run)
        block.vector(dve.run)
        block.tensor(pe.run)


_INS = ["L0_attn_x", "L0_attn_Wq", "L0_attn_bq", "L0_attn_Wk", "L0_attn_bk", "L0_attn_Wv", "L0_attn_bv",
        "L0_attn_Wo", "L0_attn_bo", "L0_ffn_w_gate", "L0_ffn_w_shared_up", "L0_ffn_w_shared_down",
        "L0_ffn_w_up", "L0_ffn_w_down"]
_OUTS = [((1, 2048, 512), "float32")]


def kernel(**inputs):
    import concourse.bacc as _bacc
    from concourse.bass_utils import run_bass_kernel_spmd as _run

    nc = _bacc.Bacc("TRN2", target_bir_lowering=False, num_devices=1)
    arrays, args = {}, []
    for name in _INS:
        a = np.asarray(inputs[name])
        if name in ("L0_attn_bq", "L0_attn_bk"):
            a = a.reshape(-1, P).T
        a = np.ascontiguousarray(a)
        arrays[f"in_{name}"] = a
        args.append(nc.dram_tensor(f"in_{name}", a.shape, mybir.dt.from_np(a.dtype), kind="ExternalInput").ap())
    for i, (shape, dtype) in enumerate(_OUTS):
        dt = mybir.dt.from_np(np.dtype(dtype))
        args.append(nc.dram_tensor(f"out_{i}", shape, dt, kind="ExternalOutput").ap())
    build(nc, *args)
    r = _run(nc, [arrays], core_ids=[0])
    return r.results[0]["out_0"]
```

```python
from contextlib import ExitStack
from itertools import zip_longest

import numpy as np

import concourse.bass as bass
from concourse import mybir

F32 = mybir.dt.float32
F32R = mybir.dt.float32r
BF16 = mybir.dt.bfloat16
U32 = mybir.dt.uint32
ALU = mybir.AluOpType
ACT = mybir.ActivationFunctionType
AX = mybir.AxisListType

P = 128
BANK = 512


class Counter:

    def __init__(self, handle):
        self.handle, self.count = handle, 0

    def add(self, n):
        self.count += n
        return (self, self.count)


class Queue:

    def __init__(self):
        self.ops, self.seen = [], {}

    def wait(self, *marks):
        for mark in marks:
            if mark is None:
                continue
            counter, value = mark
            if self.seen.get(id(counter), 0) < value:
                self.seen[id(counter)] = value
                self.ops.append(lambda e, h=counter.handle, v=value: e.wait_ge(h, v))

    def do(self, op, counter=None, by=1):
        if counter is None:
            self.ops.append(op)
            return None
        self.ops.append(lambda e, h=counter.handle: op(e).then_inc(h, by))
        return counter.add(by)

    def run(self, e):
        for op in self.ops:
            op(e)


def build(nc, x, Wq, bq, Wk, bk, Wv, bv, Wo, bo, w_gate, w_sup, w_sdown, w_up, w_down, out):
    _, T, C = x.shape
    D = 64
    H = C // D
    SCALE = float(np.sqrt(8.0))
    E = w_gate.shape[1]
    HE = w_down.shape[1]
    HS = w_sdown.shape[0]
    TOPK, CAP, EPS = 6, 256, 1e-5
    KC = C // P
    NT = T // P
    QC = 256
    QT = QC // P
    NCH = T // QC
    HALF = T // 2
    KT4 = T // P // 4
    SKIP = 1 << 17

    ctx = ExitStack()
    with ctx:
        def sb(name, shape, dt=F32, stack=ctx):
            return stack.enter_context(nc.sbuf_tensor(name, shape, dt))

        def counter(name):
            return Counter(ctx.enter_context(nc.semaphore(name)))

        def hbm(name, shape, dt=F32):
            return nc.dram_tensor(name, shape, dt).ap()

        q_hbm = hbm("q_hbm", (H // 2, 2, P, T))
        x1_hbm = hbm("x1_hbm", (T, C))
        disp_hbm = hbm("disp_hbm", (E * CAP, C))
        y_hbm = hbm("y_hbm", (E * CAP, C))

        slots = [ctx.enter_context(nc.psum_tensor(f"slot{i}", [P, 2 * BANK], F32)) for i in range(3)]
        pv_acc = ctx.enter_context(nc.psum_tensor("pv_acc", [P, BANK], F32))
        misc = ctx.enter_context(nc.psum_tensor("misc", [P, BANK], F32))
        slot_free = [[], [], []]
        slot_turn = [0]

        def take_slot():
            i = slot_turn[0] % 3
            slot_turn[0] += 1
            return i, slots[i]

        ident = sb("ident", [P, P])
        slot_of = sb("slot_of", [P, NT, TOPK], U32)
        weight_of = sb("weight_of", [P, NT, TOPK])
        half_neg = sb("half_neg", [P, 1])
        att = ExitStack()
        rows_first = ExitStack()
        stage = [sb(f"stage{i}", [P, 2, C], F32, rows_first) for i in range(4)]
        stage_gap = sb("stage_gap", [P, 4, T], F32, rows_first)
        stage += [sb(f"stage{i}", [P, 2, C], F32, rows_first) for i in range(4, NT // 2)]
        rows_first.close()
        k_stack = sb("k_stack", [P, H, T], F32R, att)
        early = ExitStack()
        w_raw = [None] + [sb(f"w_raw{i}", [P, KC, C], F32, early) for i in (1, 2)]
        raw_k = ExitStack()
        w_raw[0] = sb("w_raw0", [P, KC, C], F32, raw_k)
        raw_k.close()
        q_hi = [sb("q_hi0", [P, 2 * BANK], F32R, early)]
        q_lo = [sb("q_lo0", [P, 2 * BANK], F32R, early)]
        q_hi.append(sb("q_hi1", [P, 2 * BANK], F32R, early))
        q_lo.append(sb("q_lo1", [P, 2 * BANK], F32R, early))
        x_lo = sb("x_lo", [P, NT, KC, P], F32R, early)
        early.close()
        v_pair = sb("v_pair", [P, NT, H, P], F32R, att)
        wo_sb = sb("wo_sb", [P, KC, C], F32, att)
        wg_sb = sb("wg_sb", [P, KC, E], F32, att)
        bo_all = sb("bo_all", [P, C], F32, att)
        before = sb("before", [P, P], BF16, att)
        ones_bf = sb("ones_bf", [P, P], BF16, att)
        iota_e = sb("iota_e", [P, E], F32, att)
        count_so_far = sb("count_so_far", [P, E], BF16, att)
        pro = ExitStack()
        x_hi = sb("x_hi", [P, NT, KC, P], F32R, pro)
        w_hi, w_lo = [None] * 2, [None] * 2
        w_hi[0], w_lo[0] = (sb(name, [P, KC, C], F32R, pro) for name in ("w_hi0", "w_lo0"))
        v_rows = ExitStack()
        v_gap = sb("v_gap", [P, 2, C], F32, v_rows)
        v_plain = [sb(f"v_plain{i}", [P, 2, C], F32, v_rows) for i in range(2)]
        v_rows.close()
        w_hi[1], w_lo[1] = (sb(name, [P, KC, C], F32R, pro) for name in ("w_hi1", "w_lo1"))
        zeros = sb("zeros", [P, C // 2], F32, pro)
        bias_k = sb("bias_k", [P, KC], F32, pro)
        bias_q = sb("bias_q", [P, KC], F32, pro)
        pro.close()
        prob = sb("prob", [P, 2, QT, T], F32, att)
        p_hi = [sb(f"p_hi{i}", [P, 4, QC], F32R, att) for i in range(2)]
        p_lo = [sb(f"p_lo{i}", [P, 4, QC], F32R, att) for i in range(2)]
        q_stack = [sb(f"q_stack{i}", [P, 2, QC], F32R, att) for i in range(2)]
        row_min = sb("row_min", [P, 2, QT, 2], F32, att)
        row_sum = sb("row_sum", [P, 2, QT, 2], F32, att)
        row_inv = sb("row_inv", [P, QT], F32, att)
        scaled = sb("scaled", [P, QC], F32, att)
        moved = sb("moved", [P, QC], F32, att)
        feats = sb("feats", [P, H // 2, QC], F32, att)
        resid = [sb(f"resid{i}", [P, C], F32, att) for i in range(QT)]
        x1_t = sb("x1_t", [P, KC, P], F32, att)
        small = sb("small", [P, 40], F32, att)
        stats, top_sum, top_f = small[:, 0:6], small[:, 6:7], small[:, 7:13]
        place, over, slot_f = (small[:, 19 + 7 * i:19 + 7 * i + TOPK] for i in range(3))
        mean_var, rstd = (small[:, 13:15], small[:, 15:17]), (small[:, 17:18], small[:, 18:19])
        score = sb("score", [P, E], F32, att)
        top = sb("top", [P, 8], F32, att)
        top_i = sb("top_i", [P, 8], U32, att)
        onehot = x1_t[:, 0:TOPK * E // P, :].rearrange("p a b -> p (a b)").rearrange("p (k e) -> p k e", e=E)
        picked = sb("picked", [P, E], BF16, att)
        scat = sb("scat", [P, TOPK], U32, att)
        att.close()
        NB, NY = 5, 3
        rows = [sb(f"rows{i}", [P, 2, C]) for i in range(NB)]
        up_w = [sb(f"up_w{i}", [P, KC, 2 * HE]) for i in range(NB)]
        down_w = [sb(f"down_w{i}", [HE, C]) for i in range(NB)]
        sup_w = sb("sup_w", [P, KC, 2 * HS])
        sdown_w = sb("sdown_w", [HS, C])
        rows_hi = [sb(f"rows_hi{i}", [P, KC, CAP], F32R) for i in range(2)]
        rows_lo = [sb(f"rows_lo{i}", [P, KC, CAP], F32R) for i in range(2)]
        up_hi = [sb(f"up_hi{i}", [P, KC, 2 * HE], F32R) for i in range(2)]
        up_lo = [sb(f"up_lo{i}", [P, KC, 2 * HE], F32R) for i in range(2)]
        sup_hi = sb("sup_hi", [P, KC, 2 * HS], F32R)
        sup_lo = sb("sup_lo", [P, KC, 2 * HS], F32R)
        gate_e = [sb(f"gate_e{i}", [P, CAP]) for i in range(2)]
        gate_g = [sb(f"gate_g{i}", [P, CAP]) for i in range(2)]
        hid = [sb(f"hid{i}", [P, CAP]) for i in range(2)]
        y_out = [sb(f"y_out{i}", [P, 2, C]) for i in range(NY)]
        base = sb("base", [P, NT, C])
        NG, NF = 24, 4
        got = [sb(f"got{i}", [P, C]) for i in range(NG)]
        f_stats = sb("f_stats", [P, 2, 6])
        f_mv = sb("f_mv", [P, NT, 2])
        f_rstd = sb("f_rstd", [P, NT])
        final = [sb(f"final{i}", [P, C]) for i in range(NF)]

        pe, act, dve, pool, sp = Queue(), Queue(), Queue(), Queue(), Queue()

        c_pe = {n: counter(f"pe_{n}") for n in ("fill", "scores", "turned", "pv", "misc")}
        c_act = {n: counter(f"act_{n}") for n in ("hi", "exp", "misc")}
        c_dve = {n: counter(f"dve_{n}") for n in ("min", "lo", "chain")}
        c_pool = {n: counter(f"pool_{n}") for n in ("const", "chain", "lo")}
        d = {n: counter(f"dma_{n}") for n in (
            "wk", "wq", "wv", "bias", "bv", "wo", "once", "zero", "qst0", "qst1", "moved", "feats", "resid0", "resid1", "sup", "x0", "x1", "x2", "x3", "x4", "x5", "x6", "x7",
            "q0", "q1", "st", "r0", "r1", "r2", "r3", "r4", "y0", "y1", "y2", "o0", "o1", "o2", "o3")}
        d_got = [counter(f"dma_got{i}") for i in range(NG)]

        def chain(op):
            dve.wait((c_dve["chain"], c_dve["chain"].count))
            return dve.do(op, c_dve["chain"])

        def pool_chain(op):
            pool.wait((c_pool["chain"], c_pool["chain"].count))
            return pool.do(op, c_pool["chain"])

        def bank_product(dst, pairs, start=True, stop=True):
            for n, (a, b) in enumerate(pairs[:-1]):
                pe.do(lambda e, a=a, b=b, n=n: e.matmul(dst, a, b, start=start and n == 0, stop=False))
            a, b = pairs[-1]
            return lambda e: e.matmul(dst, a, b, start=start and len(pairs) == 1, stop=stop)

        pool.do(lambda e: e.memset(ident[:, :], 0.0), c_pool["const"])
        pool.wait((c_pool["const"], 1))
        ident_ready = pool.do(lambda e: e.affine_select(
            out=ident[:, :], in_=ident[:, :], compare_op=ALU.not_equal, fill=1.0, base=0,
            pattern=[[-1, P]], channel_multiplier=1), c_pool["const"])
        zeros_ready = pool.do(lambda e: e.memset(zeros[:, :], 0.0), c_pool["const"])
        pool.do(lambda e: e.memset(half_neg[:, :], -0.5))
        pool.do(lambda e: e.memset(count_so_far[:, :], 0.0))
        pool.do(lambda e: e.iota(iota_e[:, :], [[1, E]], base=0, channel_multiplier=0,
                                 allow_small_or_imprecise_dtypes=True))
        ones_ready = pool.do(lambda e: e.memset(ones_bf[:, :], 1.0), c_pool["const"])
        pool.wait(ones_ready)
        consts = pool.do(lambda e: e.affine_select(
            out=before[:, :], in_=ones_bf[:, :], compare_op=ALU.is_gt, fill=0.0, base=0,
            pattern=[[1, P]], channel_multiplier=-1), c_pool["const"])

        def w_view(w):
            return w.rearrange("(k p) n -> p k n", p=P)

        x_rows = x.rearrange("b (g t p) n -> (b g) p t n", t=2, p=P)

        def load_x(groups):
            return [sp.do(lambda e, g=g: e.dma_start(stage[g][:, :, :], x_rows[g]), d[f"x{g}"], 16) for g in groups]

        x_landed = load_x(range(2))
        wk_in = sp.do(lambda e: e.dma_start(w_raw[0][:, :, :], w_view(Wk)), d["wk"], 16)
        x_landed += load_x(range(2, NT // 2))
        for b, t in ((bk, bias_k), (bq, bias_q)):
            bias_in = sp.do(lambda e, b=b, t=t: e.dma_start(t[:, :], b), d["bias"], 16)
        wq_in = sp.do(lambda e: e.dma_start(w_raw[1][:, :, :], w_view(Wq)), d["wq"], 16)
        bv_all = wo_sb[:, 0, :]
        bv_in = sp.do(lambda e: e.dma_start(bv_all, bv.partition_broadcast(P)), d["bv"], 16)
        wv_in = sp.do(lambda e: e.dma_start(w_raw[2][:, :, :], w_view(Wv)), d["wv"], 16)

        def split_weights(i, landed, *free):
            act.wait(landed, *free)
            rounded = act.do(lambda e: e.activation(w_hi[i % 2][:, :, :], w_raw[i][:, :, :], ACT.Copy), c_act["hi"])
            dve.wait(rounded)
            return dve.do(lambda e: e.tensor_tensor(
                w_lo[i % 2][:, :, :], w_raw[i][:, :, :], w_hi[i % 2][:, :, :].bitcast(F32), ALU.subtract), c_dve["lo"])

        w_split, x_split = [], []

        def turn_x(g):
            i, slot = take_slot()
            view = slot[:, :].rearrange("p (t k q) -> p t k q", t=2, k=KC)
            pe.wait(ident_ready, x_landed[g], *slot_free[i])
            for t in range(2):
                for k in range(KC):
                    last = (lambda e, g=g, t=t, k=k, view=view: e.transpose(
                        view[:, t, k, :], stage[g][:, t, k * P:(k + 1) * P], ident[:, :]))
                    if (t, k) == (1, KC - 1):
                        x_read = pe.do(last, c_pe["fill"])
                    else:
                        pe.do(last)
            act.wait(x_read)
            tiles = slice(2 * g, 2 * g + 2)
            rounded = act.do(lambda e, view=view, tiles=tiles: e.activation(x_hi[:, tiles, :, :], view, ACT.Copy), c_act["hi"])
            dve.wait(rounded)
            x_split.append(dve.do(lambda e, view=view, tiles=tiles: e.tensor_tensor(
                x_lo[:, tiles, :, :], view, x_hi[:, tiles, :, :].bitcast(F32), ALU.subtract), c_dve["lo"]))
            slot_free[i] = [x_split[-1]]

        turn_x(0)
        turn_x(1)
        w_split.append(split_weights(0, wk_in))
        turn_x(2)
        turn_x(3)

        sp.wait(zeros_ready)
        zero_row = zeros[:, :].unsqueeze(1).to_broadcast([P, 4, C // 2])
        disp_pieces = disp_hbm.rearrange("(g p t) (u n) -> g p (t u) n", p=P, t=2, u=2)
        zero_pieces = [lambda e, g=g: e.dma_start(disp_pieces[g], zero_row) for g in range(E * CAP // (P * 2))]

        def zero_some(count):
            for _ in range(count):
                if zero_pieces:
                    sp.do(zero_pieces.pop(0), d["zero"], 16)

        q_stored = [None] * 2

        def three_products(a, b):
            return [(a[0], b[0]), (a[0], b[1]), (a[1], b[0])]

        for n_w, (name, bias) in enumerate((("k", bias_k), ("q", bias_q))):
            halves = range(T // (2 * BANK))
            for g, pair in ([(g, pair) for g in halves for pair in range(H // 2)] if name == "k" else
                            [(g, pair) for pair in range(H // 2) for g in halves]):
                if len(x_split) < NT // 2:
                    turn_x(len(x_split))
                tok = slice(g * 2 * BANK, (g + 1) * 2 * BANK)
                i, slot = take_slot()
                pe.wait(w_split[n_w], x_split[4 * g + 3], *slot_free[i])
                for n in range(2):
                    four = slice((2 * g + n) * 4, (2 * g + n + 1) * 4)
                    dst = slot[:, n * BANK:(n + 1) * BANK].rearrange("p (t q) -> p t q", t=4)
                    last = bank_product(dst, [ab for k in range(KC) for ab in three_products(
                        [w[n_w][:, k, pair * P:(pair + 1) * P] for w in (w_hi, w_lo)],
                        [xt[:, four, k, :] for xt in (x_hi, x_lo)])])
                    made = pe.do(last, c_pe["fill"])
                if name == "k":
                    zero_some(4)
                    for odd in range(2):
                        h, hi, lo = 2 * pair + odd, slice(odd * D, (odd + 1) * D), slice((1 - odd) * D, (2 - odd) * D)
                        act.wait(made, bias_in)
                        rounded = act.do(lambda e, h=h, hi=hi, slot=slot, tok=tok, bias=bias, pair=pair: e.activation(
                            k_stack[hi, h, tok], slot[hi, :], ACT.Identity, bias=bias[hi, pair:pair + 1]), c_act["hi"])
                        dve.wait(rounded)
                        slot_free[i] = [dve.do(lambda e, h=h, hi=hi, lo=lo, slot=slot, tok=tok, bias=bias, pair=pair:
                                              e.scalar_tensor_tensor(
                            out=k_stack[lo, h, tok], in0=slot[hi, :], scalar=bias[hi, pair:pair + 1],
                            in1=k_stack[hi, h, tok].bitcast(F32), op0=ALU.add, op1=ALU.subtract), c_dve["lo"])]
                else:
                    zero_some(2)
                    qh, ql = q_hi[g % 2], q_lo[g % 2]
                    act.wait(made, bias_in, q_stored[g % 2])
                    rounded = act.do(lambda e, slot=slot, bias=bias, pair=pair, qh=qh: e.activation(
                        qh[:, :], slot[:, :], ACT.Identity, bias=bias[:, pair:pair + 1]), c_act["hi"])
                    dve.wait(rounded)
                    slot_free[i] = [dve.do(lambda e, slot=slot, bias=bias, pair=pair, qh=qh, ql=ql: e.scalar_tensor_tensor(
                        out=ql[:, :], in0=slot[:, :], scalar=bias[:, pair:pair + 1],
                        in1=qh[:, :].bitcast(F32), op0=ALU.add, op1=ALU.subtract), c_dve["lo"])]
                    sp.wait(*slot_free[i])
                    for part, src in ((0, qh), (1, ql)):
                        q_stored[g % 2] = sp.do(lambda e, src=src, part=part, pair=pair, tok=tok: e.dma_start(
                            q_hbm[pair, part, :, tok], src[:, :].bitcast(F32)), d[f"qst{g % 2}"], 16)
                if (name, g, pair) == ("k", 1, 0):
                    w_split.append(split_weights(1, wq_in))
            if name == "k":
                w_split.append(split_weights(2, wv_in, made))
                for a, b in ((wg_sb[:, :, :], w_view(w_gate)),
                             (bo_all[:, :], bo.partition_broadcast(P))):
                    sp.do(lambda e, a=a, b=b: e.dma_start(a, b), d["once"], 16)

        v_split = [[], []]
        for g in range(NT // 2):
            zero_some(2)
            i, slot = take_slot()
            pe.wait(w_split[2], *slot_free[i])
            for t in range(2):
                last = bank_product(slot[:, t * BANK:(t + 1) * BANK], [ab for k in range(KC) for ab in three_products(
                    [xt[:, 2 * g + t, k, :] for xt in (x_hi, x_lo)], [w[0][:, k, :] for w in (w_hi, w_lo)])])
                made = pe.do(last, c_pe["fill"])
            vp = v_plain[g % 2]
            dve.wait(made, bv_in, *v_split[g % 2])
            added = dve.do(lambda e, slot=slot, vp=vp: e.tensor_tensor(
                vp[:, :, :], slot[:, :].rearrange("p (t n) -> p t n", t=2),
                bv_all.unsqueeze(1).to_broadcast([P, 2, C]), ALU.add), c_dve["chain"])
            slot_free[i] = [added]
            act.wait(added, *(q_stored if g == 2 else ()))
            for t in range(2):
                src = vp[:, t, :].rearrange("p (h c) -> p h c", h=H)
                rounded = act.do(lambda e, g=g, t=t, src=src: e.activation(
                    v_pair[:, 2 * g + t, :, 0:D], src, ACT.Copy), c_act["hi"])
            pool.wait(rounded)
            dve.wait(rounded)
            for t in range(2):
                src = vp[:, t, :].rearrange("p (h c) -> p h c", h=H)
                op = (lambda e, g=g, t=t, src=src: e.tensor_tensor(
                    v_pair[:, 2 * g + t, :, D:P], src, v_pair[:, 2 * g + t, :, 0:D].bitcast(F32), ALU.subtract))
                v_split[g % 2].append(dve.do(op, c_dve["lo"]) if t else pool_chain(op))

        def barrier():
            marks = [(c, c.count) for c in (*c_pe.values(), *c_act.values(), *c_dve.values(), *c_pool.values(),
                                            *d.values()) if c.count]
            for q in (pe, act, dve, pool, sp):
                q.wait(*marks)

        groups = [(c, h) for c in range(NCH) for h in range(H)]
        q_in, q_read = {}, [None] * 2
        lowest, exp_done, t_read, hi_done, lo_done, pv_read = {}, {}, {}, {}, {}, [None] * 2
        copy_read = {}
        misc_free = [None]
        pv_free = [None]

        def load_q(m):
            c, h = groups[m]
            sp.wait(q_read[m % 2])
            src = q_hbm[h // 2, :, (h % 2) * D:(h % 2 + 1) * D, c * QC:(c + 1) * QC].rearrange("s c q -> c s q")
            for half in (slice(0, D), slice(D, P)):
                q_in[m] = sp.do(lambda e, half=half: e.dma_start(q_stack[m % 2][half, :, :].bitcast(F32), src),
                                d[f"q{m % 2}"], 16)

        def scores(m, u):
            c, h = groups[m]
            half, j = divmod(u, QT)
            i, slot = take_slot()
            pe.wait(q_in[m])
            qs = q_stack[m % 2]
            for n in range(2):
                pe.wait(*slot_free[i][:n + 1])
                for part in range(2):
                    keys = slice(half * HALF + n * BANK, half * HALF + (n + 1) * BANK)
                    op = (lambda e, part=part, n=n, keys=keys: e.matmul(
                        slot[:, n * BANK:(n + 1) * BANK], qs[:, part, j * P:(j + 1) * P], k_stack[:, h, keys],
                        start=part == 0, stop=part == 1))
                    if (n, part) == (1, 1):
                        made = pe.do(op, c_pe["scores"])
                    else:
                        pe.do(op)
            q_read[m % 2] = made
            return i, slot, made

        def keep_scores(m, u, i, slot, made):
            half, j = divmod(u, QT)
            dve.wait(made, t_read.get((m - 2, half)), copy_read.get((m - 2, half)))
            first = 3.0e38 if half == 0 else row_min[:, m % 2, j, 0:1]
            if half:
                dve.wait((c_dve["min"], c_dve["min"].count))
            low = dve.do(lambda e: e.tensor_scalar(
                prob[:, m % 2, j, half * HALF:(half + 1) * HALF], slot[:, :], -1.0 / SCALE, first, ALU.mult, ALU.min,
                accum_out=row_min[:, m % 2, j, half:half + 1]), c_dve["min"])
            slot_free[i] = [low]
            lowest[m, j] = low

        def raise_exp(m, u):
            half, j = divmod(u, QT)
            act.wait(lowest[m, j])
            exp_done[m, j, half] = act.do(lambda e: e.activation(
                prob[:, m % 2, j, half * HALF:(half + 1) * HALF], prob[:, m % 2, j, half * HALF:(half + 1) * HALF],
                ACT.Exp, bias=row_min[:, m % 2, j, 1:2], scale=-1.0,
                accum_out=row_sum[:, m % 2, j, half:half + 1]), c_act["exp"])

        def turn(m, u):
            i, slot = take_slot()
            view = slot[:, :].rearrange("p (t q) -> p t q", t=4)
            pe.wait(*slot_free[i], *(exp_done[m, j, u // 2] for j in range(QT)))
            b = u % 2
            for t in range(4):
                for j in range(QT):
                    op = (lambda e, t=t, j=j: e.transpose(
                        view[:, t, j * P:(j + 1) * P], prob[:, m % 2, j, (4 * u + t) * P:(4 * u + t + 1) * P],
                        ident[:, :]))
                    if (t % 2, j) == (1, QT - 1):
                        made = pe.do(op, c_pe["turned"])
                    else:
                        pe.do(op)
                if t % 2:
                    two = slice(t - 1, t + 1)
                    act.wait(made, pv_read[b])
                    hi_done[b, t // 2] = act.do(lambda e, two=two: e.activation(
                        p_hi[b][:, two, :], view[:, two, :], ACT.Copy), c_act["hi"])
            if u % 2:
                copy = prob[:, m % 2, :, (4 * u + 2) * P:(4 * u + 4) * P]
                copied = act.do(lambda e, two=two: e.activation(copy, view[:, two, :], ACT.Copy), c_act["misc"])
                slot_free[i] = [copied]
                pool.wait(copied)
                lo_done[b, 1] = copy_read[m, u // 2] = pool.do(lambda e, two=two: e.tensor_tensor(
                    p_lo[b][:, two, :], copy, p_hi[b][:, two, :].bitcast(F32), ALU.subtract), c_pool["lo"])
            t_read[m, u // 2] = made
            return i, view

        def split_lo(u, i, view):
            b = u % 2
            for half in range(2 - u % 2):
                dve.wait(hi_done[b, half])
                two = slice(2 * half, 2 * half + 2)
                lo_done[b, half] = dve.do(lambda e, two=two: e.tensor_tensor(
                    p_lo[b][:, two, :], view[:, two, :], p_hi[b][:, two, :].bitcast(F32), ALU.subtract), c_dve["lo"])
            slot_free[i] = [lo_done[b, 0], slot_free[i][0] if u % 2 else lo_done[b, 1]]

        def times_v(m, u):
            c, h = groups[m]
            b = u % 2
            if u == 0:
                pe.wait(pv_free[0])
            for t in range(4):
                pe.wait(hi_done[b, t // 2], lo_done[b, t // 2])
                for part, src in enumerate((p_hi[b], p_lo[b])):
                    kt = 4 * u + t
                    op = (lambda e, kt=kt, t=t, part=part, src=src: e.matmul(
                        pv_acc[:, 0:QC], v_pair[:, kt, h, :], src[:, t, :], start=kt == 0 and part == 0,
                        stop=kt == NT - 1 and part == 1))
                    if (t, part) == (3, 1):
                        pv_read[b] = pe.do(op, c_pe["pv"])
                    else:
                        pe.do(op)

        inverted, inv_done = {}, {}

        def invert_sums(m):
            dve.wait(*(exp_done[m, j, 1] for j in range(QT)))
            chain(lambda e: e.tensor_tensor(row_inv[:, :], row_sum[:, m % 2, :, 0], row_sum[:, m % 2, :, 1], ALU.add))
            inverted[m] = chain(lambda e: e.reciprocal(row_inv[:, :], row_inv[:, :]))

        def spread_inverse(m):
            pe.wait(inverted[m], misc_free[0])
            for j in range(QT):
                made = pe.do(lambda e, j=j: e.transpose(
                    misc[:, j * P:(j + 1) * P], row_inv[:, j:j + 1].to_broadcast([P, P]), ident[:, :]), c_pe["misc"])
            act.wait(made, feats_done.get(m - 1))
            inv_done[m] = act.do(lambda e: e.activation(scaled[:, :], misc[:, 0:QC], ACT.Copy), c_act["misc"])
            misc_free[0] = inv_done[m]

        feats_read, feats_done, moved_done = [None], {}, [None]

        def finish_group(m):
            dve.wait(inv_done[m], pv_read[1], moved_done[0])
            pv_free[0] = done = dve.do(lambda e: e.tensor_tensor(
                scaled[:, :], pv_acc[:, 0:QC], scaled[:, :], ALU.mult), c_dve["chain"])
            sp.wait(done)
            return done, sp.do(lambda e: e.dma_start(moved[0:D, :], scaled[D:P, :]), d["moved"], 16)

        def join_halves(m, done, lo_in):
            pair, odd = divmod(groups[m][1], 2)
            target = moved[0:D, :] if odd else feats[0:D, pair, :]
            pool.wait(done, lo_in, feats_read[0])
            moved_done[0] = feats_done[m] = pool_chain(lambda e: e.tensor_tensor(
                target, scaled[0:D, :], moved[0:D, :], ALU.add))
            if odd:
                sp.wait(feats_done[m])
                moved_done[0] = feats_done[m] = sp.do(lambda e: e.dma_start(
                    feats[D:P, pair, :], target), d["feats"], 16)

        x_tiles = x.rearrange("b (t p) n -> (b t) p n", p=P)
        x1_stored, scattered, counted = [None], [None], [None]
        scat_counters = [counter("dma_scat")]
        resid_free = [[]] * QT

        resid_in, biased = {}, {}

        def load_resid(c, j):
            sp.wait(*resid_free[j])
            resid_in[j] = sp.do(lambda e: e.dma_start(resid[j][:, :], x_tiles[c * QT + j]), d[f"resid{j}"], 16)

        def bias_resid(j):
            pool.wait(resid_in[j])
            biased[j] = pool_chain(lambda e: e.tensor_tensor(resid[j][:, :], resid[j][:, :], bo_all[:, :], ALU.add))

        def chunk_end(c):
            def steps(count):
                yield from [None] * (2 * count)

            def project(j):
                pe.wait(wo_in, feats_done[c * H + H - 1], feats_done[c * H + H - 2], misc_free[0])
                made = pe.do(bank_product(misc[:, :], [
                    (feats[:, k, j * P:(j + 1) * P], wo_sb[:, k, :]) for k in range(KC)]), c_pe["misc"])
                feats_read[0] = made
                return made

            def add_resid(j, made):
                dve.wait(made, biased[j])
                misc_free[0] = chain(lambda e: e.tensor_tensor(resid[j][:, :], misc[:, :], resid[j][:, :], ALU.add))

            def measure(j):
                chain(lambda e: e.bn_stats(stats[:, :], resid[j][:, :]))
                chain(lambda e: e.bn_aggr(mean_var[j][:, :], stats[:, :]))
                return chain(lambda e: e.tensor_scalar(mean_var[j][:, 1:2], mean_var[j][:, 1:2], EPS, None, ALU.add))

            def root(j, var):
                pool.wait(var)
                return pool_chain(lambda e: e.tensor_tensor(rstd[j][:, :], mean_var[j][:, 1:2], half_neg[:, :], ALU.pow))

            def dispatch(t, j, rooted):
                dve.wait(rooted)
                x1 = resid[j]
                normed = chain(lambda e: e.tensor_scalar(
                    x1[:, :], x1[:, :], mean_var[j][:, 0:1], rstd[j][:, 0:1], ALU.subtract, ALU.mult))
                sp.wait(normed)
                stored = x1_stored[0] = sp.do(lambda e: e.dma_start(x1_hbm[t * P:(t + 1) * P, :], x1[:, :]), d["st"], 16)
                yield
                pe.wait(normed, misc_free[0])
                for k in range(KC):
                    made = pe.do(lambda e, k=k: e.transpose(
                        misc[:, k * P:(k + 1) * P], x1[:, k * P:(k + 1) * P], ident[:, :]), c_pe["misc"])
                yield
                act.wait(made, (c_dve["chain"], c_dve["chain"].count))
                misc_free[0] = flipped = act.do(lambda e: e.activation(
                    x1_t[:, :, :], misc[:, :].rearrange("p (k q) -> p k q", k=KC), ACT.Copy), c_act["misc"])
                yield
                pe.wait(flipped, misc_free[0])
                gated = made = pe.do(bank_product(misc[:, 0:E], [(x1_t[:, k, :], wg_sb[:, k, :]) for k in range(KC)]),
                                     c_pe["misc"])
                yield
                act.wait(made, (c_dve["chain"], c_dve["chain"].count))
                misc_free[0] = raised = act.do(lambda e: e.activation(score[:, :], misc[:, 0:E], ACT.Exp, scale=-1.0),
                                               c_act["misc"])
                yield from steps(1)
                dve.wait(raised)
                chain(lambda e: e.tensor_scalar(score[:, :], score[:, :], 1.0, None, ALU.add))
                chain(lambda e: e.reciprocal(score[:, :], score[:, :]))
                yield from steps(1)
                chain(lambda e: e.max(top[:, :], score[:, :]))
                chain(lambda e: e.max_index(top_i[:, :], top[:, :], score[:, :]))
                chain(lambda e: e.tensor_copy(top_f[:, :], top_i[:, 0:TOPK]))
                yield from steps(1)
                dve.wait(gated)
                chain(lambda e: e.tensor_tensor(
                    onehot[:, :, :], iota_e[:, :].unsqueeze(1).to_broadcast([P, TOPK, E]),
                    top_f[:, :].unsqueeze(2).to_broadcast([P, TOPK, E]), ALU.is_equal))
                yield from steps(1)
                dve.wait(counted[0])
                mask = chain(lambda e: e.tensor_reduce(
                    picked[:, :], onehot[:, :, :].rearrange("p k e -> p e k"), AX.X, ALU.max))
                yield from steps(1)
                chain(lambda e: e.tensor_reduce(top_sum[:, :], top[:, 0:TOPK], AX.X, ALU.add))
                chain(lambda e: e.reciprocal(top_sum[:, :], top_sum[:, :]))
                yield from steps(1)
                chain(lambda e: e.tensor_scalar(top[:, 0:TOPK], top[:, 0:TOPK], top_sum[:, 0:1], None, ALU.mult))
                yield
                pe.wait(mask, misc_free[0], counted[0])
                made = pe.do(bank_product(misc[:, 0:E], [
                    (before[:, :], picked[:, :]), (ones_bf[:, :], count_so_far[:, :])]), c_pe["misc"])
                yield
                pool.wait(made, mask)
                counted[0] = pool_chain(lambda e: e.tensor_tensor(
                    count_so_far[:, :], count_so_far[:, :], picked[:, :], ALU.add))
                dve.wait(made)
                misc_free[0] = chain(lambda e: e.tensor_tensor(
                    onehot[:, :, :], onehot[:, :, :], misc[:, 0:E].unsqueeze(1).to_broadcast([P, TOPK, E]), ALU.mult))
                yield from steps(1)
                dve.wait(scattered[0])
                chain(lambda e: e.tensor_reduce(place[:, :], onehot[:, :, :], AX.X, ALU.add))
                yield from steps(1)
                chain(lambda e: e.tensor_scalar(over[:, :], place[:, :], float(CAP), float(SKIP), ALU.is_ge, ALU.mult))
                chain(lambda e: e.scalar_tensor_tensor(out=slot_f[:, :], in0=top_f[:, :], scalar=float(CAP),
                                                       in1=place[:, :], op0=ALU.mult, op1=ALU.add))
                to_go = chain(lambda e: e.tensor_tensor(scat[:, :], slot_f[:, :], over[:, :], ALU.add))
                yield
                yield "x1_t is free"
                pool.wait(to_go, normed, (d["zero"], d["zero"].count))
                for k in range(TOPK):
                    scattered[0] = pool.do(lambda e, k=k: e.indirect_dma_start(
                        disp_hbm, bass.IndirectOffsetOnAxis(scat[:, k:k + 1], 0), x1[:, :], None,
                        bounds_check=E * CAP - 1, oob_is_err=False), scat_counters[0], 16)
                    if k == 3:
                        chain(lambda e: e.tensor_scalar(over[:, :], place[:, :], float(CAP - 1), None, ALU.min))
                        chain(lambda e: e.scalar_tensor_tensor(
                            out=slot_of[:, t, :], in0=top_f[:, :], scalar=float(CAP), in1=over[:, :],
                            op0=ALU.mult, op1=ALU.add))
                    if k == TOPK - 1:
                        chain(lambda e: e.scalar_tensor_tensor(
                            out=weight_of[:, t, :], in0=place[:, :], scalar=float(CAP), in1=top[:, 0:TOPK],
                            op0=ALU.is_lt, op1=ALU.mult))
                    resid_free[j] = [scattered[0], stored]
                    if k % 2:
                        yield from steps(1)

            yield from steps(2)
            yield
            made = project(0)
            yield
            add_resid(0, made)
            yield from steps(1)
            var = measure(0)
            yield
            made = project(1)
            yield
            add_resid(1, made)
            rooted = root(0, var)
            yield from steps(1)
            var = measure(1)
            yield from steps(1)
            first = dispatch(c * QT, 0, rooted)
            for said in first:
                yield
                if said:
                    break
                if var:
                    rooted, var = root(1, var), None
            for _ in zip_longest(first, dispatch(c * QT + 1, 1, rooted)):
                yield

        side_work = []

        def side_step():
            for work in side_work[:]:
                if next(work, "over") == "over":
                    side_work.remove(work)

        sp.wait((d["qst0"], d["qst0"].count), (d["qst1"], d["qst1"].count))
        load_q(0)
        load_q(1)
        barrier()
        wo_in = sp.do(lambda e: e.dma_start(wo_sb[:, :, :], w_view(Wo)), d["wo"], 16)
        STEPS, LAG = 4, 6
        later = []
        last = len(groups) * STEPS
        for s in range(last + LAG + 2):
            m, u = divmod(s - LAG, STEPS)
            mv, uv = divmod(s - LAG - 1, STEPS)
            if 0 <= s - LAG < last:
                turned_quad = turn(m, u)
            if s < last:
                made_scores = scores(s // STEPS, s % STEPS)
                if s % STEPS == STEPS - 1 and s // STEPS + 2 < len(groups):
                    load_q(s // STEPS + 2)
            side_step()
            if 0 <= s - LAG < last:
                split_lo(u, *turned_quad)
            if LAG < s <= last + LAG:
                times_v(mv, uv)
                if uv == STEPS - 1:
                    later.append((s + 1, lambda mv=mv, halves=finish_group(mv): join_halves(mv, *halves)))
                    chunk, head = groups[mv]
                    if head == H - 2:
                        for j, delay in ((0, 1), (1, 6)):
                            later.append((s + delay, lambda chunk=chunk, j=j: load_resid(chunk, j)))
                            later.append((s + delay + 3, lambda j=j: bias_resid(j)))
                    if head == H - 1:
                        side_work.append(chunk_end(chunk))
            if s < last:
                keep_scores(s // STEPS, s % STEPS, *made_scores)
            if 3 <= s < last + 3:
                raise_exp(*divmod(s - 3, STEPS))
            if 0 <= s - LAG < last and u == 1:
                invert_sums(m)
            for due, step in [x for x in later if x[0] == s]:
                step()
            side_step()
            if 0 <= s - LAG < last and u == 3:
                spread_inverse(m)
        for q in (act, dve, pool, sp):
            q.wait((c_pe["scores"], c_pe["scores"].count), (c_pe["pv"], c_pe["pv"].count))

        sup_in = None
        for a, b in ((sup_w[:, :, :], w_view(w_sup)), (sdown_w[:, :], w_sdown)):
            sup_in = act.do(lambda e, a=a, b=b: e.dma_start(a, b), d["sup"], 16)
        sup_split = [None]
        x1_rows = x1_hbm.rearrange("(g t p) n -> g p t n", t=2, p=P)
        disp_rows = disp_hbm.rearrange("(g t p) n -> g p t n", t=2, p=P)
        y_rows = y_hbm.rearrange("(g t p) n -> g p t n", t=2, p=P)
        items = [("shared", g) for g in range(NT // 2)] + [("expert", e) for e in range(E)]
        rows_in, rows_done, turned_in, up_split, up_done, hid_done, down_done = {}, {}, {}, {}, {}, {}, {}
        y_stored = [None] * NY
        AHEAD = NB - 1
        up_bank, up_free = [pv_acc, misc], [pv_free[0], None]

        def load_rows(n):
            kind, g = items[n]
            b = n % NB
            q = act if n < AHEAD else sp
            if n >= NB:
                q.wait(*rows_done[n - NB])
            src = x1_rows if kind == "shared" else disp_rows
            if kind == "expert":
                q.do(lambda e: e.dma_start(up_w[b][:, :, :], w_up[g].rearrange("(k p) n -> p k n", p=P)), d[f"r{b}"], 16)
                q.do(lambda e: e.dma_start(down_w[b][:, :], w_down[g]), d[f"r{b}"], 16)
                q.wait(scattered[0])
            else:
                q.wait(x1_stored[0])
            rows_in[n] = q.do(lambda e: e.dma_start(rows[b][:, :, :], src[g]), d[f"r{b}"], 16)

        def flip_rows(n):
            b = n % NB
            i, slot = take_slot()
            view = slot[:, :].rearrange("p (k t q) -> p k t q", k=KC, t=2)
            pe.wait(rows_in[n], *slot_free[i])
            for k in range(KC):
                for t in range(2):
                    made = (lambda e, k=k, t=t: e.transpose(view[:, k, t, :], rows[b][:, t, k * P:(k + 1) * P], ident[:, :]))
                    if (k, t) == (KC - 1, 1):
                        made = pe.do(made, c_pe["turned"])
                    else:
                        pe.do(made)
            rows_done[n] = [made]
            turned = slot[:, :].rearrange("p (k q) -> p k q", k=KC)
            act.wait(made, up_done.get(n - 2))
            rounded = act.do(lambda e: e.activation(rows_hi[n % 2][:, :, :], turned, ACT.Copy), c_act["hi"])
            dve.wait(rounded)
            turned_in[n] = dve.do(lambda e: e.tensor_tensor(
                rows_lo[n % 2][:, :, :], turned, rows_hi[n % 2][:, :, :].bitcast(F32), ALU.subtract), c_dve["lo"])
            slot_free[i] = [turned_in[n]]
            if items[n][0] == "expert":
                rounded = act.do(lambda e: e.activation(up_hi[n % 2][:, :, :], up_w[b][:, :, :], ACT.Copy), c_act["hi"])
                pool.wait(rounded)
                up_split[n] = pool.do(lambda e: e.tensor_tensor(
                    up_lo[n % 2][:, :, :], up_w[b][:, :, :], up_hi[n % 2][:, :, :].bitcast(F32), ALU.subtract),
                    c_pool["lo"])
                rows_done[n].append(up_split[n])

        def up(n):
            kind, _ = items[n]
            b, o = n % NB, n % 2
            pe.wait(turned_in[n])
            rows_parts = (rows_hi[o], rows_lo[o])
            if kind == "shared":
                i, bank = take_slot()
                pe.wait(sup_split[0], *slot_free[i])
                for half in range(2):
                    made = bank_product(bank[:, half * CAP:(half + 1) * CAP], [ab for k in range(KC) for ab in three_products(
                        [w[:, k, half * HS:(half + 1) * HS] for w in (sup_hi, sup_lo)],
                        [r[:, k, :] for r in rows_parts])])
                    if half:
                        up_done[n] = made = pe.do(made, c_pe["fill"])
                    else:
                        pe.do(made)
                width, gate, value = HS, bank[:, CAP:2 * CAP], bank[:, 0:CAP]
            else:
                bank = up_bank[o]
                pe.wait(up_free[o], up_split[n])
                up_done[n] = made = pe.do(bank_product(bank[:, 0:CAP], [ab for k in range(KC) for ab in three_products(
                    [w[o][:, k, :] for w in (up_hi, up_lo)], [r[:, k, :] for r in rows_parts])]), c_pe["fill"])
                width, gate, value = HE, bank[0:HE, 0:CAP], bank[HE:2 * HE, 0:CAP]
            act.wait(made, hid_done.get(n - 2))
            bent = act.do(lambda e: e.activation(gate_e[o][0:width, :], gate, ACT.Tanh, scale=0.5), c_act["exp"])
            dve.wait(bent, down_done.get(n - 2))
            chain(lambda e: e.scalar_tensor_tensor(out=gate_g[o][0:width, :], in0=gate_e[o][0:width, :], scalar=1.0,
                                                   in1=gate, op0=ALU.add, op1=ALU.mult))
            hid_done[n] = chain(lambda e: e.scalar_tensor_tensor(
                out=hid[o][0:width, :], in0=gate_g[o][0:width, :], scalar=0.5, in1=value, op0=ALU.mult, op1=ALU.mult))
            if kind == "shared":
                slot_free[i] = [hid_done[n]]
            else:
                up_free[o] = hid_done[n]

        def down(n):
            kind, g = items[n]
            b, o, y = n % NB, n % 2, n % NY
            i, slot = take_slot()
            pe.wait(hid_done[n], *slot_free[i])
            for t in range(2):
                lhs = hid[o][:, t * P:(t + 1) * P] if kind == "shared" else hid[o][0:HE, t * P:(t + 1) * P]
                rhs = sdown_w[:, :] if kind == "shared" else down_w[b][:, :]
                made = pe.do(lambda e, t=t, lhs=lhs, rhs=rhs: e.matmul(
                    slot[:, t * BANK:(t + 1) * BANK], lhs, rhs, start=True, stop=True), c_pe["fill"])
            down_done[n] = made
            rows_done[n].append(made)
            if kind == "shared":
                dve.wait(made)
                added = dve.do(lambda e: e.tensor_tensor(
                    base[:, 2 * g:2 * g + 2, :], slot[:, :].rearrange("p (t n) -> p t n", t=2), rows[b][:, :, :],
                    ALU.add), c_dve["chain"])
                slot_free[i] = [added]
                rows_done[n].append(added)
                return
            dve.wait(made, y_stored[y])
            act.wait(made, y_stored[y])
            left = dve.do(lambda e: e.tensor_copy(y_out[y][:, 0, :], slot[:, 0:BANK]), c_dve["lo"])
            right = act.do(lambda e: e.activation(y_out[y][:, 1, :], slot[:, BANK:2 * BANK], ACT.Copy), c_act["misc"])
            slot_free[i] = [left, right]
            pool.wait(left, right)
            y_stored[y] = pool.do(lambda e: e.dma_start(y_rows[g], y_out[y][:, :, :]), d[f"y{y}"], 16)

        N = len(items)
        SIDE = 4
        CLEAR = NCH - 1

        def beside(count):
            for _ in range(count):
                side_step()

        loaded = 0
        for n in range(-2, N):
            if n + 2 == CLEAR:
                while side_work:
                    side_step()
                up_free[1] = misc_free[0]
            while loaded < N and loaded <= n + AHEAD and (loaded < CLEAR or n + 2 >= CLEAR):
                load_rows(loaded)
                loaded += 1
            if n == -2:
                act.wait(sup_in)
                rounded = act.do(lambda e: e.activation(sup_hi[:, :, :], sup_w[:, :, :], ACT.Copy), c_act["hi"])
                dve.wait(rounded)
                sup_split[0] = dve.do(lambda e: e.tensor_tensor(
                    sup_lo[:, :, :], sup_w[:, :, :], sup_hi[:, :, :].bitcast(F32), ALU.subtract), c_dve["lo"])
                for due, step in later:
                    if due > s:
                        step()
            if n + 2 < N:
                flip_rows(n + 2)
            beside(3 * SIDE if n == -2 else SIDE)
            if 0 <= n + 1 < N:
                up(n + 1)
            beside(SIDE)
            if n >= 0:
                down(n)
            beside(SIDE)

        pool.wait(*((d[f"y{b}"], d[f"y{b}"].count) for b in range(NY)))
        pool.wait(*((c, c.count) for c in (*c_pe.values(), *c_act.values(), *c_dve.values(), *c_pool.values())))
        got_free, got_in = [None] * NG, {}
        out_tiles = out.rearrange("b (t p) n -> (b t) p n", p=P)

        def gather(t):
            for k in range(TOPK):
                for u in (t, t + 1):
                    g = (u * TOPK + k) % NG
                    pool.wait(got_free[g])
                    got_in[u, k] = pool.do(lambda e, g=g, k=k, u=u: e.indirect_dma_start(
                        got[g][:, :], None, y_hbm, bass.IndirectOffsetOnAxis(slot_of[:, u, k:k + 1], 0),
                        bounds_check=E * CAP - 1, oob_is_err=False), d_got[g], 16)

        def add_up(t, t2):
            summed = {t: (c_dve["chain"], c_dve["chain"].count)}
            summed[t2] = summed[t]
            for k in range(TOPK):
                for u in (t, t2):
                    g = (u * TOPK + k) % NG
                    dve.wait(got_in[u, k], summed[u])
                    got_free[g] = summed[u] = dve.do(lambda e, g=g, k=k, u=u: e.scalar_tensor_tensor(
                        out=base[:, u, :], in0=got[g][:, :], scalar=weight_of[:, u, k:k + 1], in1=base[:, u, :],
                        op0=ALU.mult, op1=ALU.add), c_dve["chain"])
            for u in (t, t2):
                chain(lambda e, u=u: e.bn_stats(f_stats[:, u % 2, :], base[:, u, :]))
                chain(lambda e, u=u: e.bn_aggr(f_mv[:, u, :], f_stats[:, u % 2, :]))
            return chain(lambda e: e.tensor_scalar(f_mv[:, t:t + 2, 1], f_mv[:, t:t + 2, 1], EPS, None, ALU.add))

        def take_root(t, var):
            pool.wait(var)
            return pool_chain(lambda e: e.tensor_tensor(
                f_rstd[:, t:t + 2], f_mv[:, t:t + 2, 1], half_neg[:, :].to_broadcast([P, 2]), ALU.pow))

        def store_normed(t, root):
            for u in (t, t + 1):
                b = u % NF
                dve.wait(root, (d[f"o{b}"], d[f"o{b}"].count))
                normed = dve.do(lambda e, u=u, b=b: e.tensor_scalar(
                    final[b][:, :], base[:, u, :], f_mv[:, u, 0:1], f_rstd[:, u:u + 1], ALU.subtract, ALU.mult),
                    c_dve["chain"])
                sp.wait(normed)
                sp.do(lambda e, u=u, b=b: e.dma_start(out_tiles[u], final[b][:, :]), d[f"o{b}"], 16)

        gather(0)
        var = None
        for t in range(0, NT, 2):
            if t:
                root = take_root(t - 2, var)
            if t + 2 < NT:
                gather(t + 2)
            var = add_up(t, t + 1)
            if t:
                store_normed(t - 2, root)
        store_normed(NT - 2, take_root(NT - 2, var))
        sp.wait(*((c, c.count) for c in (*d.values(), *d_got, *scat_counters)))

        block = ctx.enter_context(nc.Block())
        block.sync(sp.run)
        block.gpsimd(pool.run)
        block.scalar(act.run)
        block.vector(dve.run)
        block.tensor(pe.run)


_INS = ["L0_attn_x", "L0_attn_Wq", "L0_attn_bq", "L0_attn_Wk", "L0_attn_bk", "L0_attn_Wv", "L0_attn_bv",
        "L0_attn_Wo", "L0_attn_bo", "L0_ffn_w_gate", "L0_ffn_w_shared_up", "L0_ffn_w_shared_down",
        "L0_ffn_w_up", "L0_ffn_w_down"]
_OUTS = [((1, 2048, 512), "float32")]


def kernel(**inputs):
    import concourse.bacc as _bacc
    from concourse.bass_utils import run_bass_kernel_spmd as _run

    nc = _bacc.Bacc("TRN2", target_bir_lowering=False, num_devices=1)
    arrays, args = {}, []
    for name in _INS:
        a = np.asarray(inputs[name])
        if name in ("L0_attn_bq", "L0_attn_bk"):
            a = a.reshape(-1, P).T
        a = np.ascontiguousarray(a)
        arrays[f"in_{name}"] = a
        args.append(nc.dram_tensor(f"in_{name}", a.shape, mybir.dt.from_np(a.dtype), kind="ExternalInput").ap())
    for i, (shape, dtype) in enumerate(_OUTS):
        dt = mybir.dt.from_np(np.dtype(dtype))
        args.append(nc.dram_tensor(f"out_{i}", shape, dt, kind="ExternalOutput").ap())
    build(nc, *args)
    r = _run(nc, [arrays], core_ids=[0])
    return r.results[0]["out_0"]
```
